# Optimizing a Trainium2 kernel written in Bass

```python
import numpy as np
import jax
import jax.numpy as jnp

def _softmax(x, axis=-1):
    return jax.nn.softmax(x, axis=axis)

def _gelu(x):
    return jax.nn.gelu(x, approximate=True)

def _silu(x):
    return jax.nn.silu(x)

def _sigmoid(x):
    return jax.nn.sigmoid(x)

def _layernorm(x, axis=-1, eps=1e-05):
    m = jnp.mean(x, axis=axis, keepdims=True)
    v = jnp.var(x, axis=axis, keepdims=True)
    return (x - m) / jnp.sqrt(v + eps)

def _scatter_add(tgt, idx, src, axis=0):
    return tgt.at[idx].add(src)

def _segment_sum(src, seg, n):
    return jax.ops.segment_sum(src, seg, n)
kernel_name = 'mk_hybrid_d1_jaxref_r8_16ada8'

def setup_inputs(seed: int=0):
    np.random.seed(seed)
    _w = jnp.asarray

    def _L0_attn_a_setup():
        import jax, jax.numpy as jnp
        import numpy as np
        D_MODEL = 128
        N_HEADS = 16
        HEAD_DIM = D_MODEL // N_HEADS
        D_LATENT = 32
        LAMBDA_DECAY = 0.01
        TIME_STEP = 0.01
        CLAMP = 10000.0

        def _reference_tuple_inner(x, Wq, Wk, Wv, Wo, W_down_kv, W_up_k, W_up_v):
            B, S, _ = x.shape
            q = x @ Wq
            k = x @ Wk
            v = x @ Wv
            latent_kv = (k + v) @ W_down_kv
            k_rec = latent_kv @ W_up_k
            v_rec = latent_kv @ W_up_v

            def heads(t):
                return t.reshape(B, S, N_HEADS, HEAD_DIM).transpose(0, 2, 1, 3)
            qh, kh, vh = (heads(q), heads(k_rec), heads(v_rec))
            scale = 1.0 / (jnp.sqrt(jnp.float32(D_MODEL)) + 1e-08)
            scores = jnp.einsum('bhqd,bhkd->bhqk', qh, kh) * scale
            scores = jnp.clip(jnp.nan_to_num(scores, nan=-1000000000.0), -CLAMP, CLAMP)
            idx = jnp.arange(S, dtype=jnp.float32)
            decay = jnp.exp(-LAMBDA_DECAY * TIME_STEP * jnp.abs(idx[:, None] - idx[None, :]))
            scores = scores * decay[None, None, :, :]
            scores = jnp.clip(jnp.nan_to_num(scores, nan=-1000000000.0), -CLAMP, CLAMP)
            attn = jax.nn.softmax(scores, axis=-1)
            out = jnp.einsum('bhqk,bhkd->bhqd', attn, vh)
            out = out.transpose(0, 2, 1, 3).reshape(B, S, D_MODEL)
            return (out @ Wo, latent_kv)
        key = jax.random.key(seed)
        ks = jax.random.split(key, 8)
        B, S = (2, 256)

        def w(k, i, o):
            return jax.random.normal(k, (i, o), dtype=jnp.float32) * 0.02
        return {'x': jax.random.normal(ks[0], (B, S, D_MODEL), dtype=jnp.float32), 'Wq': w(ks[1], D_MODEL, D_MODEL), 'Wk': w(ks[2], D_MODEL, D_MODEL), 'Wv': w(ks[3], D_MODEL, D_MODEL), 'Wo': w(ks[4], D_MODEL, D_MODEL), 'W_down_kv': w(ks[5], D_MODEL, D_LATENT), 'W_up_k': w(ks[6], D_LATENT, D_MODEL), 'W_up_v': w(ks[7], D_LATENT, D_MODEL)}
    _L0_attn_a_in = _L0_attn_a_setup()

    def _L0_attn_b_setup():
        import jax, jax.numpy as jnp
        import numpy as np
        B, S, D = (2, 256, 128)
        H = 16
        HD = D // H
        THETA = 1000.0
        SCALE = 0.02

        def _rope(t, cos, sin):
            even = t[..., ::2]
            odd = t[..., 1::2]
            return jnp.concatenate([even * cos - odd * sin, odd * cos + even * sin], axis=-1)
        key = jax.random.key(seed)
        k0, k1, k2, k3, k4 = jax.random.split(key, 5)
        x = jax.random.normal(k0, (B, S, D), dtype=jnp.float32)
        wq = SCALE * jax.random.normal(k1, (D, D), dtype=jnp.float32)
        wk = SCALE * jax.random.normal(k2, (D, HD), dtype=jnp.float32)
        wv = SCALE * jax.random.normal(k3, (D, HD), dtype=jnp.float32)
        wo = SCALE * jax.random.normal(k4, (D, D), dtype=jnp.float32)
        return {'x': x, 'wq': wq, 'wk': wk, 'wv': wv, 'wo': wo}
    _L0_attn_b_in = _L0_attn_b_setup()

    def _L0_ffn_setup():
        import jax, jax.numpy as jnp
        import numpy as np
        DIM = 128

        def _reference_tuple_inner(x, W_r, W_k, W_v, mu_r, mu_k):
            B, T, C = x.shape
            x_prev = jnp.concatenate([jnp.zeros((B, 1, C), x.dtype), x[:, :-1, :]], axis=1)
            xr = mu_r * x + (1.0 - mu_r) * x_prev
            xk = mu_k * x + (1.0 - mu_k) * x_prev
            r = jax.nn.sigmoid(jnp.einsum('btc,dc->btd', xr, W_r))
            k = jnp.einsum('btc,dc->btd', xk, W_k)
            k_act = jnp.square(jax.nn.relu(k))
            out = r * jnp.einsum('btc,dc->btd', k_act, W_v)
            new_state = x[:, -1, :]
            return (out, new_state)
        key = jax.random.key(seed)
        ks = jax.random.split(key, 6)
        B, T, C = (8, 256, DIM)
        x = jax.random.normal(ks[0], (B, T, C), dtype=jnp.float32)
        s = 1.0 / np.sqrt(C)
        W_r = jax.random.uniform(ks[1], (C, C), jnp.float32, -s, s)
        W_k = jax.random.uniform(ks[2], (C, C), jnp.float32, -s, s)
        W_v = jax.random.uniform(ks[3], (C, C), jnp.float32, -s, s)
        mu_r = jax.random.uniform(ks[4], (C,), jnp.float32)
        mu_k = jax.random.uniform(ks[5], (C,), jnp.float32)
        return {'x': x, 'W_r': W_r, 'W_k': W_k, 'W_v': W_v, 'mu_r': mu_r, 'mu_k': mu_k}
    _L0_ffn_in = _L0_ffn_setup()
    _d = {'L0_attn_a_x': _L0_attn_a_in['x'], 'L0_attn_a_Wq': _L0_attn_a_in['Wq'], 'L0_attn_a_Wk': _L0_attn_a_in['Wk'], 'L0_attn_a_Wv': _L0_attn_a_in['Wv'], 'L0_attn_a_Wo': _L0_attn_a_in['Wo'], 'L0_attn_a_W_down_kv': _L0_attn_a_in['W_down_kv'], 'L0_attn_a_W_up_k': _L0_attn_a_in['W_up_k'], 'L0_attn_a_W_up_v': _L0_attn_a_in['W_up_v'], 'L0_attn_b_wq': _L0_attn_b_in['wq'], 'L0_attn_b_wk': _L0_attn_b_in['wk'], 'L0_attn_b_wv': _L0_attn_b_in['wv'], 'L0_attn_b_wo': _L0_attn_b_in['wo'], 'L0_ffn_W_r': _L0_ffn_in['W_r'], 'L0_ffn_W_k': _L0_ffn_in['W_k'], 'L0_ffn_W_v': _L0_ffn_in['W_v'], 'L0_ffn_mu_r': _L0_ffn_in['mu_r'], 'L0_ffn_mu_k': _L0_ffn_in['mu_k']}
    _x0 = _d['L0_attn_a_x']
    _d['L0_attn_a_x'] = jax.random.normal(jax.random.fold_in(jax.random.key(seed), 1), (8, 512, 128), dtype=_x0.dtype)
    del _x0
    return _d

def reference(L0_attn_a_x, L0_attn_a_Wq, L0_attn_a_Wk, L0_attn_a_Wv, L0_attn_a_Wo, L0_attn_a_W_down_kv, L0_attn_a_W_up_k, L0_attn_a_W_up_v, L0_attn_b_wq, L0_attn_b_wk, L0_attn_b_wv, L0_attn_b_wo, L0_ffn_W_r, L0_ffn_W_k, L0_ffn_W_v, L0_ffn_mu_r, L0_ffn_mu_k):

    def _L0_attn_a_ref(x, Wq, Wk, Wv, Wo, W_down_kv, W_up_k, W_up_v):
        import jax, jax.numpy as jnp
        import numpy as np
        D_MODEL = 128
        N_HEADS = 16
        HEAD_DIM = D_MODEL // N_HEADS
        D_LATENT = 32
        LAMBDA_DECAY = 0.01
        TIME_STEP = 0.01
        CLAMP = 10000.0

        def _reference_tuple_inner(x, Wq, Wk, Wv, Wo, W_down_kv, W_up_k, W_up_v):
            B, S, _ = x.shape
            q = x @ Wq
            k = x @ Wk
            v = x @ Wv
            latent_kv = (k + v) @ W_down_kv
            k_rec = latent_kv @ W_up_k
            v_rec = latent_kv @ W_up_v

            def heads(t):
                return t.reshape(B, S, N_HEADS, HEAD_DIM).transpose(0, 2, 1, 3)
            qh, kh, vh = (heads(q), heads(k_rec), heads(v_rec))
            scale = 1.0 / (jnp.sqrt(jnp.float32(D_MODEL)) + 1e-08)
            scores = jnp.einsum('bhqd,bhkd->bhqk', qh, kh) * scale
            scores = jnp.clip(jnp.nan_to_num(scores, nan=-1000000000.0), -CLAMP, CLAMP)
            idx = jnp.arange(S, dtype=jnp.float32)
            decay = jnp.exp(-LAMBDA_DECAY * TIME_STEP * jnp.abs(idx[:, None] - idx[None, :]))
            scores = scores * decay[None, None, :, :]
            scores = jnp.clip(jnp.nan_to_num(scores, nan=-1000000000.0), -CLAMP, CLAMP)
            attn = jax.nn.softmax(scores, axis=-1)
            out = jnp.einsum('bhqk,bhkd->bhqd', attn, vh)
            out = out.transpose(0, 2, 1, 3).reshape(B, S, D_MODEL)
            return (out @ Wo, latent_kv)
        return _reference_tuple_inner(x, Wq, Wk, Wv, Wo, W_down_kv, W_up_k, W_up_v)[0]

    def _L0_attn_b_ref(x, wq, wk, wv, wo):
        import jax, jax.numpy as jnp
        import numpy as np
        B, S, D = (2, 256, 128)
        H = 16
        HD = D // H
        THETA = 1000.0
        SCALE = 0.02

        def _rope(t, cos, sin):
            even = t[..., ::2]
            odd = t[..., 1::2]
            return jnp.concatenate([even * cos - odd * sin, odd * cos + even * sin], axis=-1)
        b, s, d = x.shape
        freqs = 1.0 / THETA ** (jnp.arange(0, HD, 2, dtype=jnp.float32) / HD)
        ang = jnp.arange(s, dtype=jnp.float32)[:, None] * freqs[None, :]
        cos, sin = (jnp.cos(ang), jnp.sin(ang))
        q = (x @ wq.T).reshape(b, s, H, HD).transpose(0, 2, 1, 3)
        k = x @ wk
        v = x @ wv
        q = _rope(q, cos[None, None], sin[None, None])
        k = _rope(k, cos[None], sin[None])
        scores = jnp.einsum('bhqd,bkd->bhqk', q, k) / np.float32(np.sqrt(HD))
        causal = jnp.triu(jnp.ones((s, s), dtype=bool), 1)
        scores = jnp.where(causal[None, None], -jnp.inf, scores)
        w = jax.nn.softmax(scores, axis=-1)
        out = jnp.einsum('bhqk,bkd->bhqd', w, v)
        out = out.transpose(0, 2, 1, 3).reshape(b, s, d)
        return out @ wo.T

    def _L0_ffn_ref(x, W_r, W_k, W_v, mu_r, mu_k):
        import jax, jax.numpy as jnp
        import numpy as np
        DIM = 128

        def _reference_tuple_inner(x, W_r, W_k, W_v, mu_r, mu_k):
            B, T, C = x.shape
            x_prev = jnp.concatenate([jnp.zeros((B, 1, C), x.dtype), x[:, :-1, :]], axis=1)
            xr = mu_r * x + (1.0 - mu_r) * x_prev
            xk = mu_k * x + (1.0 - mu_k) * x_prev
            r = jax.nn.sigmoid(jnp.einsum('btc,dc->btd', xr, W_r))
            k = jnp.einsum('btc,dc->btd', xk, W_k)
            k_act = jnp.square(jax.nn.relu(k))
            out = r * jnp.einsum('btc,dc->btd', k_act, W_v)
            new_state = x[:, -1, :]
            return (out, new_state)
        return _reference_tuple_inner(x, W_r, W_k, W_v, mu_r, mu_k)[0]
    x = L0_attn_a_x
    x = x + _L0_attn_a_ref(_layernorm(x, axis=-1), L0_attn_a_Wq, L0_attn_a_Wk, L0_attn_a_Wv, L0_attn_a_Wo, L0_attn_a_W_down_kv, L0_attn_a_W_up_k, L0_attn_a_W_up_v)
    x = x + _L0_ffn_ref(_layernorm(x, axis=-1), L0_ffn_W_r, L0_ffn_W_k, L0_ffn_W_v, L0_ffn_mu_r, L0_ffn_mu_k)
    x = x + _L0_attn_b_ref(_layernorm(x, axis=-1), L0_attn_b_wq, L0_attn_b_wk, L0_attn_b_wv, L0_attn_b_wo)
    x = x + _L0_ffn_ref(_layernorm(x, axis=-1), L0_ffn_W_r, L0_ffn_W_k, L0_ffn_W_v, L0_ffn_mu_r, L0_ffn_mu_k)
    return x

_drawn_inputs = setup_inputs


def setup_inputs(seed=0):
    import zlib

    import numpy as np

    out = dict(_drawn_inputs(seed))
    spreads = {}
    factors = {'L0_attn_a_Wq': 8.0,
     'L0_attn_a_Wk': 8.0,
     'L0_attn_a_Wv': 8.0,
     'L0_attn_a_Wo': 8.0,
     'L0_attn_a_W_down_kv': 8.0,
     'L0_attn_a_W_up_k': 8.0,
     'L0_attn_a_W_up_v': 8.0,
     'L0_attn_b_wq': 8.0,
     'L0_attn_b_wk': 8.0,
     'L0_attn_b_wv': 8.0,
     'L0_attn_b_wo': 8.0,
     'L0_ffn_mu_r': 12.088}
    for name, (base, spread) in spreads.items():
        noise = np.random.default_rng([zlib.crc32(name.encode()), seed]).standard_normal(out[name].shape)
        drawn = base * np.exp(spread * noise) if base else spread * noise
        out[name] = jnp.asarray(drawn.astype(out[name].dtype))
    for name, factor in factors.items():
        out[name] = (out[name] * factor).astype(out[name].dtype)
    return out
```

```python
import numpy as np
import concourse.bass as bass
import concourse.mybir as mybir
from contextlib import ExitStack

F32 = mybir.dt.float32
ALU = mybir.AluOpType
ACT = mybir.ActivationFunctionType
AX = mybir.AxisListType

P = 128
B, S = 8, 512
TILES = S // P
H, HD = 16, 8
LAT = 32
CLAMP = 10000.0
EPS = 1e-5
SCALE_A = float(np.float32(1.0) / (np.sqrt(np.float32(P)) + np.float32(1e-8)))
SCALE_B = float(np.float32(1.0) / np.float32(np.sqrt(HD)))

WEIGHTS = ["wq_a", "wk_a", "wv_a", "wo_a", "w_down", "w_up_k", "w_up_v", "wq_b", "wq_b_swapped",
           "wk_b", "wk_b_swapped", "wv_b", "wo_b", "w_r", "w_k", "w_v", "mu_r", "mu_k"]
TABLES = ["identity", "head_mask", "decay", "causal", "rope_cos", "rope_sin"]


def build(nc, dram, out):
    with ExitStack() as ctx:
        def sb(name, shape, dt=F32):
            return ctx.enter_context(nc.sbuf_tensor(name, shape, dt))

        def bank(name):
            return ctx.enter_context(nc.psum_tensor(name, [P, 512], F32))

        def sem(name):
            return ctx.enter_context(nc.semaphore(name))

        X = sb("residual", [P, B, TILES, P])
        w = {n: sb(n + "_sb", list(dram[n].shape)) for n in WEIGHTS + TABLES}
        w_sum = sb("w_sum", [P, P])
        w_sum_t = sb("w_sum_t", [P, P])
        w_lat_t = sb("w_lat_t", [LAT, P])
        w_kk = sb("w_kk", [P, P])
        w_vv = sb("w_vv", [P, P])
        mu_rest = sb("mu_rest", [P, 2])
        half = sb("minus_half", [P, TILES])
        stats = sb("stats", [P, TILES, 6])
        mean_sum, mean_dif, m2_sum, mean, dif_sq, var_p, var_eps = [
            sb(n, [P, TILES]) for n in "mean_sum mean_dif m2_sum mean dif_sq var_p var_eps".split()]
        rstd = sb("rstd", [P, TILES])
        normed = sb("normed", [P, TILES, P])
        xt = sb("xt", [P, 1 + S])
        q_t = sb("q_t", [P, S])
        k_t = sb("k_t", [P, S])
        rot = sb("rot", [P, S])
        v_sb = sb("v_sb", [P, TILES, P])
        q_head = sb("q_head", [P, S])
        w1 = sb("w1", [P, S])
        w2 = sb("w2", [P, S])
        row_max = sb("row_max", [P, 1])
        neg_max = sb("neg_max", [P, 1])
        probs = sb("probs", [P, S])
        probs_t = sb("probs_t", [P, TILES, P])
        row_sum = sb("row_sum", [P, 1])
        row_inv = sb("row_inv", [P, 1])
        o_sb = sb("o_sb", [P, TILES, P])
        o_t = sb("o_t", [P, S])
        mix_r = sb("mix_r", [P, S])
        mix_k = sb("mix_k", [P, S])
        part_r = sb("part_r", [P, S])
        part_k = sb("part_k", [P, S])
        relu_k = sb("relu_k", [P, S])
        act_k = sb("act_k", [P, S])
        gate = sb("gate", [P, S])
        gated = sb("gated", [P, S])

        ps_t, ps_q, ps_k, ps_v, ps_q2, ps_k2, ps_s, ps_o = [
            bank("ps_" + n) for n in ("t", "q", "k", "v", "q2", "k2", "s", "o")]

        loaded = sem("loaded")
        x_loaded = sem("x_loaded")
        names = ("const_ready zeroed w_summed w_sum_tr w_sum_copied lat_done lat_copied kv_folded kv_copied "
                 "stats_done parts_done squares_done var_sum_done var_done rstd_done normed_done xt_done xt_copied "
                 "proj_done rot_step proj_copied head_picked scores_done w_step weighted max_done "
                 "exp_done pt_done pt_copied sum_step o_done o_scaled ot_done ot_copied wo_done "
                 "x_done mix_step mixed k_done relu_done k_acted ffn_done gate_done gated_done stored")
        s = {n: sem(n) for n in names.split()}
        block = ctx.enter_context(nc.Block())

        N_LOADS = len(WEIGHTS) + len(TABLES)
        PHASES = ["a", "ffn", "b", "ffn"]
        ATT = {0: 0, 2: 1}
        FFN = {1: 0, 3: 1}

        @block.sync
        def _(sp):
            for t in WEIGHTS + TABLES:
                sp.dma_start(w[t][:], dram[t]).then_inc(loaded, 16)
            sp.dma_start(X[:], dram["x"].rearrange("b (t p) d -> p b t d", p=P)).then_inc(x_loaded, 16)
            sp.wait_ge(s["x_done"], 4 * B)
            sp.dma_start(out.rearrange("b (t p) d -> p b t d", p=P), X[:]).then_inc(s["stored"], 16)
            sp.wait_ge(s["stored"], 16)

        @block.gpsimd
        def _(pool):
            pool.memset(half[:], -0.5).then_inc(s["const_ready"], 1)
            pool.wait_ge(s["const_ready"], 1)
            for phase in range(4):
                with pool.Fori(0, B) as b:
                    n = b + (phase * B + 1)
                    pool.wait_ge(s["var_done"], n)
                    pool.tensor_tensor(rstd[:], var_eps[:], half[:], ALU.pow).then_inc(s["rstd_done"], 1)

        @block.scalar
        def _(act):
            for phase in range(4):
                with act.Fori(0, B) as b:
                    if phase in ATT:
                        with act.Fori(0, H) as h:
                            for qt in range(TILES):
                                m = ((ATT[phase] * B + b) * H + h) * TILES + (qt + 1)
                                act.wait_ge(s["max_done"], m)
                                act.activation(probs[:], w2[:], ACT.Exp, bias=neg_max[:]).then_inc(s["exp_done"], 1)
                    else:
                        act.wait_ge(s["ffn_done"], b + (FFN[phase] * B + 1))
                        act.activation(gate[:], ps_q[:], ACT.Tanh, scale=0.5).then_inc(s["gate_done"], 1)

        @block.tensor
        def _(pe):
            ident = w["identity"]
            pe.wait_ge(loaded, 16 * N_LOADS)
            pe.wait_ge(s["w_summed"], 1)
            pe.transpose(ps_t[:, 0:P], w_sum[:], ident[:]).then_inc(s["w_sum_tr"], 1)
            pe.wait_ge(s["w_sum_copied"], 1)
            pe.matmul(ps_q[0:LAT, 0:P], w["w_down"][:], w_sum_t[:], start=True, stop=True).then_inc(s["lat_done"], 1)
            pe.wait_ge(s["lat_copied"], 1)
            pe.matmul(ps_k[:, 0:P], w_lat_t[:], w["w_up_k"][:], start=True, stop=True)
            pe.matmul(ps_v[:, 0:P], w_lat_t[:], w["w_up_v"][:], start=True, stop=True).then_inc(s["kv_folded"], 1)
            pe.wait_ge(s["kv_copied"], 1)

            def transposed(n):
                pe.wait_ge(s["normed_done"], n)
                for t in range(TILES):
                    last = pe.transpose(ps_t[:, t * P:(t + 1) * P], normed[:, t, :], ident[:])
                last.then_inc(s["xt_done"], 1)

            for phase in range(4):
                with pe.Fori(0, B) as b:
                    n = b + (phase * B + 1)
                    transposed(n)
                    if phase in ATT:
                        a = ATT[phase]
                        na = b + (a * B + 1)
                        pe.wait_ge(s["xt_copied"], n)
                        xs = xt[:, 1:1 + S]
                        wq, wk = (w["wq_a"], w_kk) if a == 0 else (w["wq_b"], w["wk_b"])
                        wv, nv = (w_vv, P) if a == 0 else (w["wv_b"], HD)
                        pe.matmul(ps_q[:], wq[:], xs, start=True, stop=True)
                        pe.matmul(ps_k[:], wk[:], xs, start=True, stop=True)
                        if a:
                            pe.matmul(ps_q2[:], w["wq_b_swapped"][:], xs, start=True, stop=True)
                            pe.matmul(ps_k2[:], w["wk_b_swapped"][:], xs, start=True, stop=True)
                        for t in range(TILES):
                            last = pe.matmul(ps_v[:, t * P:t * P + nv], xt[:, 1 + t * P:1 + (t + 1) * P], wv[:],
                                             start=True, stop=True)
                        last.then_inc(s["proj_done"], 1)
                        with pe.Fori(0, H) as h:
                            pe.wait_ge(s["proj_copied"], na)
                            pe.wait_ge(s["head_picked"], (a * B + b) * H + h + 1)
                            for qt in range(TILES):
                                m = ((a * B + b) * H + h) * TILES + (qt + 1)
                                pe.matmul(ps_s[:], q_head[:, qt * P:(qt + 1) * P], k_t[:], start=True, stop=True)\
                                  .then_inc(s["scores_done"], 1)
                                pe.wait_ge(s["exp_done"], m)
                                for t in range(TILES):
                                    last = pe.transpose(ps_t[:, t * P:(t + 1) * P], probs[:, t * P:(t + 1) * P], ident[:])
                                last.then_inc(s["pt_done"], 1)
                                pe.wait_ge(s["pt_copied"], m)
                                for t in range(TILES):
                                    v = v_sb[:, t, bass.ds(h * HD, HD)] if a == 0 else v_sb[:, t, 0:HD]
                                    last = pe.matmul(ps_o[:, 0:HD], probs_t[:, t, :], v,
                                                     start=(t == 0), stop=(t == TILES - 1))
                                last.then_inc(s["o_done"], 1)
                                pe.wait_ge(s["o_scaled"], m)
                        for t in range(TILES):
                            last = pe.transpose(ps_t[:, t * P:(t + 1) * P], o_sb[:, t, :], ident[:])
                        last.then_inc(s["ot_done"], 1)
                        pe.wait_ge(s["ot_copied"], na)
                        wo = w["wo_a"] if a == 0 else w["wo_b"]
                        for t in range(TILES):
                            last = pe.matmul(ps_v[:, t * P:(t + 1) * P], o_t[:, t * P:(t + 1) * P], wo[:],
                                             start=True, stop=True)
                        last.then_inc(s["wo_done"], 1)
                    else:
                        nf = b + (FFN[phase] * B + 1)
                        pe.wait_ge(s["mixed"], nf)
                        pe.matmul(ps_k[:], w["w_k"][:], mix_k[:], start=True, stop=True).then_inc(s["k_done"], 1)
                        for t in range(TILES):
                            pe.matmul(ps_q[:, t * P:(t + 1) * P], mix_r[:, t * P:(t + 1) * P], w["w_r"][:],
                                      start=True, stop=True)
                        pe.wait_ge(s["k_acted"], nf)
                        for t in range(TILES):
                            last = pe.matmul(ps_v[:, t * P:(t + 1) * P], act_k[:, t * P:(t + 1) * P], w["w_v"][:],
                                             start=True, stop=True)
                        last.then_inc(s["ffn_done"], 1)

        @block.vector
        def _(dve):
            dve.memset(xt[:, 0:1], 0.0).then_inc(s["zeroed"], 1)
            dve.memset(v_sb[:], 0.0).then_inc(s["zeroed"], 1)
            dve.wait_ge(loaded, 16 * N_LOADS)
            dve.tensor_tensor(w_sum[:], w["wk_a"][:], w["wv_a"][:], ALU.add).then_inc(s["w_summed"], 1)
            for i, mu in enumerate(("mu_r", "mu_k")):
                dve.tensor_scalar(mu_rest[:, i:i + 1], w[mu][:], -1.0, 1.0, ALU.mult, ALU.add).then_inc(s["zeroed"], 1)
            dve.wait_ge(s["w_sum_tr"], 1)
            dve.tensor_copy(w_sum_t[:], ps_t[:, 0:P]).then_inc(s["w_sum_copied"], 1)
            dve.wait_ge(s["lat_done"], 1)
            dve.tensor_copy(w_lat_t[:], ps_q[0:LAT, 0:P]).then_inc(s["lat_copied"], 1)
            dve.wait_ge(s["kv_folded"], 1)
            dve.tensor_copy(w_kk[:], ps_k[:, 0:P])
            dve.tensor_copy(w_vv[:], ps_v[:, 0:P]).then_inc(s["kv_copied"], 1)
            dve.wait_ge(s["zeroed"], 4)
            dve.wait_ge(s["kv_copied"], 1)
            dve.wait_ge(x_loaded, 16)

            for phase in range(4):
                with dve.Fori(0, B) as b:
                    n = b + (phase * B + 1)
                    if phase:
                        dve.wait_ge(s["x_done"], n - B)
                    for t in range(TILES):
                        last = dve.bn_stats(stats[:, t, :], X[:, b, t, :])
                    last.then_inc(s["stats_done"], 1)
                    even, odd = stats[:, :, 1], stats[:, :, 4]
                    dve.wait_ge(s["stats_done"], n)
                    dve.tensor_tensor(mean_sum[:], even, odd, ALU.add)
                    dve.tensor_tensor(mean_dif[:], even, odd, ALU.subtract)
                    dve.tensor_tensor(m2_sum[:], stats[:, :, 2], stats[:, :, 5], ALU.add).then_inc(s["parts_done"], 1)
                    dve.wait_ge(s["parts_done"], n)
                    dve.tensor_scalar(mean[:], mean_sum[:], 0.5, None, ALU.mult)
                    dve.tensor_tensor(dif_sq[:], mean_dif[:], mean_dif[:], ALU.mult).then_inc(s["squares_done"], 1)
                    dve.wait_ge(s["squares_done"], n)
                    dve.scalar_tensor_tensor(var_p[:], dif_sq[:], P / 4, m2_sum[:], ALU.mult, ALU.add)\
                       .then_inc(s["var_sum_done"], 1)
                    dve.wait_ge(s["var_sum_done"], n)
                    dve.tensor_scalar(var_eps[:], var_p[:], 1 / P, EPS, ALU.mult, ALU.add).then_inc(s["var_done"], 1)
                    dve.wait_ge(s["rstd_done"], n)
                    for t in range(TILES):
                        last = dve.tensor_scalar(normed[:, t, :], X[:, b, t, :], mean[:, t:t + 1], rstd[:, t:t + 1],
                                                 ALU.subtract, ALU.mult)
                    last.then_inc(s["normed_done"], 1)
                    dve.wait_ge(s["xt_done"], n)
                    dve.tensor_copy(xt[:, 1:1 + S], ps_t[:]).then_inc(s["xt_copied"], 1)
                    if phase in ATT:
                        a = ATT[phase]
                        na = b + (a * B + 1)
                        dve.wait_ge(s["proj_done"], na)
                        if a == 0:
                            dve.tensor_copy(q_t[:], ps_q[:])
                            dve.tensor_copy(k_t[:], ps_k[:])
                            dve.tensor_copy(v_sb[:].rearrange("p t d -> p (t d)"), ps_v[:]).then_inc(s["proj_copied"], 1)
                        else:
                            c, sn = w["rope_cos"], w["rope_sin"]
                            k0 = b * 4
                            dve.tensor_tensor(q_t[:], ps_q[:], c[:], ALU.mult)
                            dve.tensor_tensor(rot[:], ps_q2[:], sn[:], ALU.mult).then_inc(s["rot_step"], 1)
                            dve.wait_ge(s["rot_step"], k0 + 1)
                            dve.tensor_tensor(q_t[:], q_t[:], rot[:], ALU.add).then_inc(s["rot_step"], 1)
                            dve.wait_ge(s["rot_step"], k0 + 2)
                            dve.tensor_tensor(k_t[:], ps_k[:], c[:], ALU.mult)
                            dve.tensor_tensor(rot[:], ps_k2[:], sn[:], ALU.mult).then_inc(s["rot_step"], 1)
                            dve.wait_ge(s["rot_step"], k0 + 3)
                            dve.tensor_tensor(k_t[:], k_t[:], rot[:], ALU.add).then_inc(s["rot_step"], 1)
                            dve.tensor_copy(v_sb[:, :, 0:HD], ps_v[:].rearrange("p (t d) -> p t d", d=P)[:, :, 0:HD])\
                               .then_inc(s["proj_copied"], 1)
                        with dve.Fori(0, H) as h:
                            dve.wait_ge(s["proj_copied"], na)
                            mh = (a * B + b) * H + h
                            dve.tensor_scalar(q_head[:], q_t[:], w["head_mask"][:, bass.ds(h, 1)], None, ALU.mult)\
                               .then_inc(s["head_picked"], 1)
                            for qt in range(TILES):
                                m = mh * TILES + (qt + 1)
                                dve.wait_ge(s["scores_done"], m)
                                if a == 0:
                                    dve.tensor_scalar(w1[:], ps_s[:], SCALE_A, -CLAMP, ALU.mult, ALU.max)\
                                       .then_inc(s["w_step"], 1)
                                    dve.wait_ge(s["w_step"], m)
                                    dve.scalar_tensor_tensor(w2[:], w1[:], CLAMP, w["decay"][:, qt, :], ALU.min, ALU.mult)\
                                       .then_inc(s["weighted"], 1)
                                else:
                                    dve.scalar_tensor_tensor(w2[:], ps_s[:], SCALE_B, w["causal"][:, qt, :],
                                                             ALU.mult, ALU.min).then_inc(s["weighted"], 1)
                                dve.wait_ge(s["weighted"], m)
                                dve.reduce_max(row_max[:], w2[:], AX.X).then_inc(s["sum_step"], 1)
                                dve.wait_ge(s["sum_step"], m * 3 - 2)
                                dve.tensor_scalar(neg_max[:], row_max[:], -1.0, None, ALU.mult).then_inc(s["max_done"], 1)
                                dve.wait_ge(s["exp_done"], m)
                                dve.reduce_sum(row_sum[:], probs[:], AX.X).then_inc(s["sum_step"], 1)
                                dve.wait_ge(s["sum_step"], m * 3 - 1)
                                dve.reciprocal(row_inv[:], row_sum[:]).then_inc(s["sum_step"], 1)
                                dve.wait_ge(s["pt_done"], m)
                                dve.tensor_copy(probs_t[:].rearrange("p t d -> p (t d)"), ps_t[:]).then_inc(s["pt_copied"], 1)
                                dve.wait_ge(s["o_done"], m)
                                dve.wait_ge(s["sum_step"], m * 3)
                                dve.tensor_scalar(o_sb[:, qt, bass.ds(h * HD, HD)], ps_o[:, 0:HD], row_inv[:], None,
                                                  ALU.mult).then_inc(s["o_scaled"], 1)
                        dve.wait_ge(s["ot_done"], na)
                        dve.tensor_copy(o_t[:], ps_t[:]).then_inc(s["ot_copied"], 1)
                        dve.wait_ge(s["wo_done"], na)
                        dve.tensor_tensor(X[:, b, :, :].rearrange("p t d -> p (t d)"), ps_v[:],
                                          X[:, b, :, :].rearrange("p t d -> p (t d)"), ALU.add).then_inc(s["x_done"], 1)
                    else:
                        nf = b + (FFN[phase] * B + 1)
                        dve.wait_ge(s["xt_copied"], n)
                        dve.tensor_scalar(part_r[:], xt[:, 0:S], mu_rest[:, 0:1], None, ALU.mult)
                        dve.tensor_scalar(part_k[:], xt[:, 0:S], mu_rest[:, 1:2], None, ALU.mult).then_inc(s["mix_step"], 1)
                        dve.wait_ge(s["mix_step"], nf)
                        dve.scalar_tensor_tensor(mix_r[:], xt[:, 1:1 + S], w["mu_r"][:], part_r[:], ALU.mult, ALU.add)
                        dve.scalar_tensor_tensor(mix_k[:], xt[:, 1:1 + S], w["mu_k"][:], part_k[:], ALU.mult, ALU.add)\
                           .then_inc(s["mixed"], 1)
                        dve.wait_ge(s["k_done"], nf)
                        dve.tensor_scalar(relu_k[:], ps_k[:], 0.0, None, ALU.max).then_inc(s["relu_done"], 1)
                        dve.wait_ge(s["relu_done"], nf)
                        dve.tensor_tensor(act_k[:], relu_k[:], relu_k[:], ALU.mult).then_inc(s["k_acted"], 1)
                        dve.wait_ge(s["gate_done"], nf)
                        dve.scalar_tensor_tensor(gated[:], gate[:], 1.0, ps_v[:], ALU.add, ALU.mult)\
                           .then_inc(s["gated_done"], 1)
                        dve.wait_ge(s["gated_done"], nf)
                        xb = X[:, b, :, :].rearrange("p t d -> p (t d)")
                        dve.scalar_tensor_tensor(xb, gated[:], 0.5, xb, ALU.mult, ALU.add).then_inc(s["x_done"], 1)


def tables():
    i = np.arange(S, dtype=np.float32)
    dist = np.abs(i[:, None] - i[None, :])
    decay = np.exp(np.float32(-0.01 * 0.01) * dist).astype(np.float32)
    causal = np.where(i[:, None] >= i[None, :], np.float32(3.0e38), np.float32(-3.0e38)).astype(np.float32)
    freqs = (np.float32(1.0) / np.float32(1000.0) ** (np.arange(0, HD, 2, dtype=np.float32) / np.float32(HD)))
    ang = i[None, :] * freqs[:, None].astype(np.float32)
    cos, sin = np.cos(ang), np.sin(ang)
    rows = np.arange(P)
    by_tile = lambda m: np.ascontiguousarray(m.reshape(TILES, P, S).transpose(1, 0, 2))
    return {
        "identity": np.eye(P, dtype=np.float32),
        "head_mask": (rows[:, None] // HD == np.arange(H)[None, :]).astype(np.float32),
        "decay": by_tile(decay),
        "causal": by_tile(causal),
        "rope_cos": np.tile(np.concatenate([cos, cos]), (H, 1)).astype(np.float32),
        "rope_sin": np.tile(np.concatenate([-sin, sin]), (H, 1)).astype(np.float32),
    }


def kernel(**inputs):
    import concourse.bacc as bacc
    from concourse.bass_utils import run_bass_kernel_spmd

    x = {k.removeprefix("L0_"): np.ascontiguousarray(v) for k, v in inputs.items()}
    split = np.array([*range(0, HD, 2), *range(1, HD, 2)])
    swap = np.array([*range(1, HD, 2), *range(0, HD, 2)])
    heads = (np.arange(H) * HD)[:, None]
    wq_b = x["attn_b_wq"].T
    wk_b = x["attn_b_wk"]
    arrays = {
        "x": x["attn_a_x"], "wq_a": x["attn_a_Wq"], "wk_a": x["attn_a_Wk"], "wv_a": x["attn_a_Wv"],
        "wo_a": x["attn_a_Wo"], "w_down": x["attn_a_W_down_kv"], "w_up_k": x["attn_a_W_up_k"],
        "w_up_v": x["attn_a_W_up_v"],
        "wq_b": wq_b[:, (heads + split).ravel()], "wq_b_swapped": wq_b[:, (heads + swap).ravel()],
        "wk_b": np.tile(wk_b[:, split], (1, H)), "wk_b_swapped": np.tile(wk_b[:, swap], (1, H)),
        "wv_b": x["attn_b_wv"], "wo_b": x["attn_b_wo"].T,
        "w_r": x["ffn_W_r"].T, "w_k": x["ffn_W_k"].T, "w_v": x["ffn_W_v"].T,
        "mu_r": x["ffn_mu_r"].reshape(P, 1), "mu_k": x["ffn_mu_k"].reshape(P, 1),
        **tables(),
    }
    arrays = {k: np.ascontiguousarray(v) for k, v in arrays.items()}
    nc = bacc.Bacc("TRN2", target_bir_lowering=False, num_devices=1)
    dram = {k: nc.dram_tensor(k + "_dram", v.shape, mybir.dt.from_np(v.dtype), kind="ExternalInput").ap()
            for k, v in arrays.items()}
    out = nc.dram_tensor("out_0_dram", (B, S, P), F32, kind="ExternalOutput").ap()
    build(nc, dram, out)
    result = run_bass_kernel_spmd(nc, [{k + "_dram": v for k, v in arrays.items()}], core_ids=[0])
    return result.results[0]["out_0_dram"]
```

```python
import numpy as np
import concourse.bass as bass
import concourse.mybir as mybir
from contextlib import ExitStack

F32 = mybir.dt.float32
BF16 = mybir.dt.bfloat16
I32 = mybir.dt.int32
ALU = mybir.AluOpType
ACT = mybir.ActivationFunctionType
AX = mybir.AxisListType

P = 128
B, S = 8, 512
TILES = S // P
H, HD = 16, 8
LAT = 32
HALF = H // 2
GROUPS = 4
CLAMP = 10000.0
EPS = 1e-5
DECAY = 0.01 * 0.01
LIMIT = 60.0
SCALE_A = float(np.float32(1.0) / (np.sqrt(np.float32(P)) + np.float32(1e-8)))
SCALE_B = float(np.float32(1.0) / np.float32(np.sqrt(HD)))

Q_PARTS = (0, 0, 0, 1, 1, 2)
K_PARTS = (0, 1, 2, 0, 1, 0)
TERMS = len(Q_PARTS)
STACK = 72
QM, QP, KP, KM = range(4)
PARTS_OF = {QM: Q_PARTS, QP: Q_PARTS, KP: K_PARTS, KM: K_PARTS}

UP_K, UP_V = 0, 1
PACK_FIRST = [("identity", P), ("wk_a", P), ("wv_a", P), ("w_down", LAT), ("wq_a", P)]
PACK_FOLD = [("fold_down", S), ("fold_up", S)]
PACK_REST = [("wo_a", P), ("wq_b", P), ("wq_b_swapped", P), ("wk_b", P), ("wk_b_swapped", P), ("wv_b", HD),
             ("wo_b", P), ("w_r", P), ("w_k", P), ("w_v", P), ("mu_r", 1), ("mu_k", 1),
             ("diag_decay", P), ("diag_causal", P), ("head_mask", H), ("rope_cos", S), ("rope_sin", S)]
PACKS = {"first": PACK_FIRST, "fold": PACK_FOLD, "rest": PACK_REST}


class Job:

    def __init__(self, kind, it, step, first):
        self.kind, self.it, self.step, self.first = kind, it, step, first
        self.chunks = 32 if kind == "A" else 24

    def at(self, per, base):
        fixed = self.first * per + base
        return fixed if self.it is None else self.it * (self.step * per) + fixed

    def n(self, more=0):
        return self.at(1, (0 if self.kind == "A" else B) + more)

    def burst(self, more=0):
        return self.at(8, (0 if self.kind == "A" else 8 * B) + more)

    def chunk(self, more=0):
        return self.at(self.chunks, (0 if self.kind == "A" else 32 * B) + more)

    def aux(self, more=0):
        return self.at(AUX_PER_JOB[self.kind], AUX_BASE[self.kind] + more)

    @property
    def known(self):
        return self.first + (0 if self.kind == "A" else B)

    def slot_of(self, c):
        return (self.first * self.chunks + (0 if self.kind == "A" else 32 * B) + c) % 3


def pre_kind(n):
    return None if n == 2 * B - 1 else "A" if n < B - 1 else "B"


def aux_steps(n):
    nxt = pre_kind(n)
    if nxt == "A":
        steps = [(0, "a", "norms"), (0, "b", "pre_xt"), (1, "a", "q"), (1, "b", "k"), (3, "b", "v"), (5, "a", "o_first")]
        post = [(2, "a", "o_second"), (2, "b", "o_t"), (3, "a", "wo"), (4, "b", "post_xt"),
                (5, "b", "ffn_k"), (6, "a", "ffn_r"), (6, "b", "ffn_v")]
    else:
        steps = [(0, "a", "norms"), (5, "b", "o_first")]
        post = [(2, "a", "o_second"), (2, "b", "o_t"), (3, "b", "wo"), (5, "a", "post_xt"),
                (6, "a", "ffn_k"), (6, "b", "ffn_r"), (7, "a", "ffn_v")]
    if nxt == "B":
        steps += [(0, "b", "pre_xt"), (1, "a", "k"), (1, "b", "k_swapped"), (3, "a", "q"), (4, "a", "q_swapped"),
                  (4, "b", "v")]
    return sorted(steps + (post if n else []))


AUX_PROLOGUE = ["w_sum_t", "w_lat_t", "w_kk", "w_vv", "pre_xt", "q", "k", "v"]
AUX_TAIL = ["o_second", "o_t", "wo", "post_xt", "ffn_k", "ffn_r", "ffn_v"]


def aux_before(n):
    return len(AUX_PROLOGUE) + sum(len(aux_steps(m)) for m in range(n))


GENERAL_SEMS = """x_loaded tables_loaded stats_done parts_done squares_done var_sum_done var_done rstd_done normed_done
    xt_done xt_copied proj_done rot_step proj_copied head_picked scores_done w_step weighted sum_step max_done
    exp_done pt_done pt_copied o_done o_scaled ot_done ot_copied wo_done x_done mix_step mixed k_done relu_done
    k_acted ffn_done gate_done gated_done stored""".split()

AUX_PER_JOB = {"A": len(aux_steps(1)), "B": len(aux_steps(B + 1))}
AUX_BASE = {"A": aux_before(1) - AUX_PER_JOB["A"], "B": aux_before(B)}


def aux_index(job, name):
    k = [s[2] for s in aux_steps(job.known)].index(name)
    return aux_before(0) + k if job.known == 0 else job.aux(k)


def build(nc, dram, out):
    with ExitStack() as ctx:
        def sb(name, shape, dt=F32):
            return ctx.enter_context(nc.sbuf_tensor(name, shape, dt))

        def sem(name):
            return ctx.enter_context(nc.semaphore(name))

        X = sb("residual", [P, B, TILES, P])
        packs, w = {}, {}
        for pack, members in PACKS.items():
            packs[pack] = sb("pack_" + pack, [P, sum(c for _, c in members)])
            at = 0
            for name, cols in members:
                w[name] = packs[pack][:, at:at + cols]
                at += cols
        w_up = sb("w_up", [LAT, 2, P])
        norm_sum = sb("norm_sum", [P, 32], BF16)
        w_sum = sb("w_sum", [P, P])
        w_sum_t = sb("w_sum_t", [P, P])
        w_lat_t = sb("w_lat_t", [LAT, P])
        w_kk = sb("w_kk", [P, P])
        w_vv = sb("w_vv", [P, P])
        mu_rest = sb("mu_rest", [P, 2])
        minus_half = sb("minus_half", [P, TILES])
        one = sb("one", [P, 1])

        ln_names = "mean_sum mean_dif m2_sum mean dif_sq var_p var_eps rstd".split()
        ln = {side: {n: sb(f"{side}_{n}", [P, TILES]) for n in ln_names} for side in ("pre", "post")}
        for side in ("pre", "post"):
            ln[side]["stats"] = sb(side + "_stats", [P, TILES, 6])
            ln[side]["normed"] = sb(side + "_normed", [P, TILES, P])
            ln[side]["xt"] = sb(side + "_xt", [P, 1 + S])

        folded = [sb(f"folded_{v}", [P, S]) for v in range(4)]
        rest = [sb(f"rest_{v}", [P, S]) for v in range(2)]
        parts = [sb(f"parts_{v}", [P, 3, S], BF16) for v in range(4)]
        stacks = [sb(f"stack_{v}", [STACK, 2, HALF, S], BF16) for v in range(4)]
        squares = sb("squares", [P, 2, S], BF16)
        norms = sb("norms", [64, 2 * B])
        v_stage = sb("v_stage", [P, TILES, P])
        v_heads = sb("v_heads", [P, 2, TILES, HALF, 32])
        probs = sb("probs", [P, 2, GROUPS, 2 * S])
        o_raw = sb("o_raw", [P, 2, S])
        inv_sum = sb("inv_sum", [P, TILES * GROUPS, 2])
        o_tok = sb("o_tok", [P, TILES, P])
        o_t = sb("o_t", [P, S])
        part_r, part_k, mix_r, mix_k, relu_k, act_k, gate, gated = [
            sb(n, [P, S]) for n in "part_r part_k mix_r mix_k relu_k act_k gate gated".split()]
        norm_rows = sb("norm_rows", [1, 3, 32 * 2 * B])
        flag_f = sb("flag_f", [1, 1])
        flag = sb("flag", [1, 1], I32)

        psum = ctx.enter_context(nc.psum_tensor("scores", [P, 3 * 1024], F32))
        slots = [psum[:, 1024 * i:1024 * (i + 1)] for i in range(3)]
        o_bank = ctx.enter_context(nc.psum_tensor("o_bank", [P, S], F32))
        aux = ctx.enter_context(nc.psum_tensor("aux_bank", [P, S], F32))

        loaded = {pack: sem("loaded_" + pack) for pack in PACKS}
        up_loaded, x_first, x_rest = sem("up_loaded"), sem("x_first"), sem("x_rest")
        tables_loaded = sem("tables_loaded")
        pool_consts, dve_consts, mu_ready = sem("pool_consts"), sem("dve_consts"), sem("mu_ready")
        w_summed = sem("w_summed")
        scores_done = sem("scores_done")
        diag_done = sem("diag_done")
        exp_done = sem("exp_done")
        products_done = sem("products_done")
        aux_filled = sem("aux_filled")
        aux_emptied = sem("aux_emptied")
        o_copied = sem("o_copied")
        roped = {QM: sem("roped_q"), KP: sem("roped_k")}
        part_step = [sem(f"part_step_{v}") for v in range(4)]
        parts_done = [sem(f"parts_done_{v}") for v in range(4)]
        stacked = [[sem(f"stacked_{v}_{half}") for half in range(2)] for v in range(4)]
        squared = sem("squared")
        stacks_zeroed = sem("stacks_zeroed")
        v_placed = [sem("v_placed_0"), sem("v_placed_1")]
        lns = {side: {n: sem(f"{side}_{n}_done") for n in ("stats", "parts", "squares", "var_sum", "var", "rstd", "normed")}
               for side in ("pre", "post")}
        inv_done = sem("inv_done")
        prev_scaled_k, prev_scaled_r, mixed_k, mixed_r = sem("prev_scaled_k"), sem("prev_scaled_r"), sem("mixed_k"), sem("mixed_r")
        k_acted = sem("k_acted")
        x_done = sem("x_done")
        stored = sem("stored")
        passed = {engine: sem("passed_" + engine) for engine in ("pool", "sync", "vector")}
        norms_moved, bound_step, flag_done = sem("norms_moved"), sem("bound_step"), sem("flag_done")
        general_sems = {n: sem("g_" + n) for n in GENERAL_SEMS}
        block = ctx.enter_context(nc.Block())

        def xb(b):
            return X[:, b, :, :].rearrange("p t d -> p (t d)")

        def tail_copied(name):
            return aux_before(2 * B) + AUX_TAIL.index(name) + 1

        def copied(job, name):
            return aux_index(job, name) + 1

        def loops(eng, body):
            body(Job("A", None, 1, 0))
            with eng.Fori(0, 2) as it:
                for r in range(3):
                    body(Job("A", it, 3, 1 + r))
            body(Job("A", None, 1, B - 1))
            body(Job("B", None, 1, 0))
            with eng.Fori(0, B - 2) as it:
                body(Job("B", it, 1, 1))
            body(Job("B", None, 1, B - 1))

        def general(eng, program):
            eng.wait_ge(flag_done, 1)
            needed = eng.value_load(flag[0:1, 0:1], min_val=0, max_val=1)
            with eng.If(needed):
                program(eng)

        def slot_groups(kind, u):
            if kind == "A" or u % 2 == 0:
                return (0, 1, 2), (3,)
            return (0, 1), ()

        def chunk_in_job(kind, u, c):
            return 4 * u + c if kind == "A" else 6 * (u // 2) + 4 * (u % 2) + c

        s = general_sems
        ATT = {0: 0, 2: 1}
        FFN = {1: 0, 3: 1}
        ident = w["identity"]
        g = {"decay": probs[:, 0, :, 0:S], "causal": probs[:, 0, :, S:2 * S]}
        stats, normed, xt = ln["pre"]["stats"], ln["pre"]["normed"], ln["post"]["xt"]
        mean_sum, mean_dif, m2_sum, mean, dif_sq, var_p, var_eps, rstd = [ln["pre"][n] for n in ln_names]
        q_t, k_t, rot, q_head = folded
        w1, w2 = rest
        v_sb = v_stage
        g_probs, relu_g = part_r, relu_k
        probs_t = probs[:, 1, 0, 0:S].rearrange("p (t d) -> p t d", d=P)
        row_max, neg_max, row_sum, row_inv = [inv_sum[:, i, 0:1] for i in range(4)]
        o_sb = o_tok
        ps_t, ps_q, ps_k, ps_v, ps_q2, ps_k2 = [psum[:, S * i:S * (i + 1)] for i in range(6)]
        ps_s, ps_o = o_bank[:], aux

        def head_mask(h):
            at = sum(cols for name, cols in PACK_REST[:[m[0] for m in PACK_REST].index("head_mask")])
            return packs["rest"][:, bass.ds(h + at, 1)]

        def general_sync(sp):
            sp.dma_start(g["decay"], dram["decay"]).then_inc(s["tables_loaded"], 16)
            sp.dma_start(g["causal"], dram["causal"]).then_inc(s["tables_loaded"], 16)
            sp.dma_start(X[:], dram["x"].rearrange("b (t p) d -> p b t d", p=P)).then_inc(s["x_loaded"], 16)
            sp.wait_ge(s["x_done"], 4 * B)
            sp.dma_start(out.rearrange("b (t p) d -> p b t d", p=P), X[:]).then_inc(s["stored"], 16)
            sp.wait_ge(s["stored"], 16)

        def general_pool(pool):
            for phase in range(4):
                with pool.Fori(0, B) as b:
                    n = b + (phase * B + 1)
                    pool.wait_ge(s["var_done"], n)
                    pool.tensor_tensor(rstd[:], var_eps[:], minus_half[:], ALU.pow).then_inc(s["rstd_done"], 1)

        def general_act(act):
            for phase in range(4):
                with act.Fori(0, B) as b:
                    if phase in ATT:
                        with act.Fori(0, H) as h:
                            for qt in range(TILES):
                                m = ((ATT[phase] * B + b) * H + h) * TILES + (qt + 1)
                                act.wait_ge(s["max_done"], m)
                                act.activation(g_probs[:], w2[:], ACT.Exp, bias=neg_max).then_inc(s["exp_done"], 1)
                    else:
                        act.wait_ge(s["ffn_done"], b + (FFN[phase] * B + 1))
                        act.activation(gate[:], ps_q, ACT.Tanh, scale=0.5).then_inc(s["gate_done"], 1)

        def general_pe(pe):
            def transposed(n):
                pe.wait_ge(s["normed_done"], n)
                for t in range(TILES):
                    last = pe.transpose(ps_t[:, t * P:(t + 1) * P], normed[:, t, :], ident)
                last.then_inc(s["xt_done"], 1)

            for phase in range(4):
                with pe.Fori(0, B) as b:
                    n = b + (phase * B + 1)
                    transposed(n)
                    if phase in ATT:
                        a = ATT[phase]
                        na = b + (a * B + 1)
                        pe.wait_ge(s["xt_copied"], n)
                        xs = xt[:, 1:1 + S]
                        wq, wk = (w["wq_a"], w_kk[:]) if a == 0 else (w["wq_b"], w["wk_b"])
                        wv, nv = (w_vv[:], P) if a == 0 else (w["wv_b"], HD)
                        pe.matmul(ps_q, wq, xs, start=True, stop=True)
                        pe.matmul(ps_k, wk, xs, start=True, stop=True)
                        if a:
                            pe.matmul(ps_q2, w["wq_b_swapped"], xs, start=True, stop=True)
                            pe.matmul(ps_k2, w["wk_b_swapped"], xs, start=True, stop=True)
                        for t in range(TILES):
                            last = pe.matmul(ps_v[:, t * P:t * P + nv], xt[:, 1 + t * P:1 + (t + 1) * P], wv,
                                             start=True, stop=True)
                        last.then_inc(s["proj_done"], 1)
                        with pe.Fori(0, H) as h:
                            pe.wait_ge(s["proj_copied"], na)
                            pe.wait_ge(s["head_picked"], (a * B + b) * H + h + 1)
                            for qt in range(TILES):
                                m = ((a * B + b) * H + h) * TILES + (qt + 1)
                                pe.matmul(ps_s, q_head[:, qt * P:(qt + 1) * P], k_t[:], start=True, stop=True)\
                                  .then_inc(s["scores_done"], 1)
                                pe.wait_ge(s["exp_done"], m)
                                for t in range(TILES):
                                    last = pe.transpose(ps_t[:, t * P:(t + 1) * P], g_probs[:, t * P:(t + 1) * P], ident)
                                last.then_inc(s["pt_done"], 1)
                                pe.wait_ge(s["pt_copied"], m)
                                for t in range(TILES):
                                    v = v_sb[:, t, bass.ds(h * HD, HD)] if a == 0 else v_sb[:, t, 0:HD]
                                    last = pe.matmul(ps_o[:, 0:HD], probs_t[:, t, :], v,
                                                     start=(t == 0), stop=(t == TILES - 1))
                                last.then_inc(s["o_done"], 1)
                                pe.wait_ge(s["o_scaled"], m)
                        for t in range(TILES):
                            last = pe.transpose(ps_t[:, t * P:(t + 1) * P], o_sb[:, t, :], ident)
                        last.then_inc(s["ot_done"], 1)
                        pe.wait_ge(s["ot_copied"], na)
                        wo = w["wo_a"] if a == 0 else w["wo_b"]
                        for t in range(TILES):
                            last = pe.matmul(ps_v[:, t * P:(t + 1) * P], o_t[:, t * P:(t + 1) * P], wo,
                                             start=True, stop=True)
                        last.then_inc(s["wo_done"], 1)
                    else:
                        nf = b + (FFN[phase] * B + 1)
                        pe.wait_ge(s["mixed"], nf)
                        pe.matmul(ps_k, w["w_k"], mix_k[:], start=True, stop=True).then_inc(s["k_done"], 1)
                        for t in range(TILES):
                            pe.matmul(ps_q[:, t * P:(t + 1) * P], mix_r[:, t * P:(t + 1) * P], w["w_r"],
                                      start=True, stop=True)
                        pe.wait_ge(s["k_acted"], nf)
                        for t in range(TILES):
                            last = pe.matmul(ps_v[:, t * P:(t + 1) * P], act_k[:, t * P:(t + 1) * P], w["w_v"],
                                             start=True, stop=True)
                        last.then_inc(s["ffn_done"], 1)

        def general_dve(dve):
            dve.wait_ge(s["tables_loaded"], 32)
            dve.wait_ge(s["x_loaded"], 16)
            for phase in range(4):
                with dve.Fori(0, B) as b:
                    n = b + (phase * B + 1)
                    if phase:
                        dve.wait_ge(s["x_done"], n - B)
                    for t in range(TILES):
                        last = dve.bn_stats(stats[:, t, :], X[:, b, t, :])
                    last.then_inc(s["stats_done"], 1)
                    even, odd = stats[:, :, 1], stats[:, :, 4]
                    dve.wait_ge(s["stats_done"], n)
                    dve.tensor_tensor(mean_sum[:], even, odd, ALU.add)
                    dve.tensor_tensor(mean_dif[:], even, odd, ALU.subtract)
                    dve.tensor_tensor(m2_sum[:], stats[:, :, 2], stats[:, :, 5], ALU.add).then_inc(s["parts_done"], 1)
                    dve.wait_ge(s["parts_done"], n)
                    dve.tensor_scalar(mean[:], mean_sum[:], 0.5, None, ALU.mult)
                    dve.tensor_tensor(dif_sq[:], mean_dif[:], mean_dif[:], ALU.mult).then_inc(s["squares_done"], 1)
                    dve.wait_ge(s["squares_done"], n)
                    dve.scalar_tensor_tensor(var_p[:], dif_sq[:], P / 4, m2_sum[:], ALU.mult, ALU.add)\
                       .then_inc(s["var_sum_done"], 1)
                    dve.wait_ge(s["var_sum_done"], n)
                    dve.tensor_scalar(var_eps[:], var_p[:], 1 / P, EPS, ALU.mult, ALU.add).then_inc(s["var_done"], 1)
                    dve.wait_ge(s["rstd_done"], n)
                    for t in range(TILES):
                        last = dve.tensor_scalar(normed[:, t, :], X[:, b, t, :], mean[:, t:t + 1], rstd[:, t:t + 1],
                                                 ALU.subtract, ALU.mult)
                    last.then_inc(s["normed_done"], 1)
                    dve.wait_ge(s["xt_done"], n)
                    dve.tensor_copy(xt[:, 1:1 + S], ps_t).then_inc(s["xt_copied"], 1)
                    if phase in ATT:
                        a = ATT[phase]
                        na = b + (a * B + 1)
                        dve.wait_ge(s["proj_done"], na)
                        if a == 0:
                            dve.tensor_copy(q_t[:], ps_q)
                            dve.tensor_copy(k_t[:], ps_k)
                            dve.tensor_copy(v_sb[:].rearrange("p t d -> p (t d)"), ps_v).then_inc(s["proj_copied"], 1)
                        else:
                            c, sn = w["rope_cos"], w["rope_sin"]
                            k0 = b * 4
                            dve.tensor_tensor(q_t[:], ps_q, c, ALU.mult)
                            dve.tensor_tensor(rot[:], ps_q2, sn, ALU.mult).then_inc(s["rot_step"], 1)
                            dve.wait_ge(s["rot_step"], k0 + 1)
                            dve.tensor_tensor(q_t[:], q_t[:], rot[:], ALU.add).then_inc(s["rot_step"], 1)
                            dve.wait_ge(s["rot_step"], k0 + 2)
                            dve.tensor_tensor(k_t[:], ps_k, c, ALU.mult)
                            dve.tensor_tensor(rot[:], ps_k2, sn, ALU.mult).then_inc(s["rot_step"], 1)
                            dve.wait_ge(s["rot_step"], k0 + 3)
                            dve.tensor_tensor(k_t[:], k_t[:], rot[:], ALU.add).then_inc(s["rot_step"], 1)
                            dve.tensor_copy(v_sb[:, :, 0:HD], ps_v.rearrange("p (t d) -> p t d", d=P)[:, :, 0:HD])\
                               .then_inc(s["proj_copied"], 1)
                        with dve.Fori(0, H) as h:
                            dve.wait_ge(s["proj_copied"], na)
                            mh = (a * B + b) * H + h
                            dve.tensor_scalar(q_head[:], q_t[:], head_mask(h), None, ALU.mult)\
                               .then_inc(s["head_picked"], 1)
                            for qt in range(TILES):
                                m = mh * TILES + (qt + 1)
                                dve.wait_ge(s["scores_done"], m)
                                if a == 0:
                                    dve.tensor_scalar(w1[:], ps_s, SCALE_A, -CLAMP, ALU.mult, ALU.max)\
                                       .then_inc(s["w_step"], 1)
                                    dve.wait_ge(s["w_step"], m)
                                    dve.scalar_tensor_tensor(w2[:], w1[:], CLAMP, g["decay"][:, qt, :], ALU.min, ALU.mult)\
                                       .then_inc(s["weighted"], 1)
                                else:
                                    dve.scalar_tensor_tensor(w2[:], ps_s, SCALE_B, g["causal"][:, qt, :],
                                                             ALU.mult, ALU.min).then_inc(s["weighted"], 1)
                                dve.wait_ge(s["weighted"], m)
                                dve.reduce_max(row_max, w2[:], AX.X).then_inc(s["sum_step"], 1)
                                dve.wait_ge(s["sum_step"], m * 3 - 2)
                                dve.tensor_scalar(neg_max, row_max, -1.0, None, ALU.mult).then_inc(s["max_done"], 1)
                                dve.wait_ge(s["exp_done"], m)
                                dve.reduce_sum(row_sum, g_probs[:], AX.X).then_inc(s["sum_step"], 1)
                                dve.wait_ge(s["sum_step"], m * 3 - 1)
                                dve.reciprocal(row_inv, row_sum).then_inc(s["sum_step"], 1)
                                dve.wait_ge(s["pt_done"], m)
                                dve.tensor_copy(probs[:, 1, 0, 0:S], ps_t).then_inc(s["pt_copied"], 1)
                                dve.wait_ge(s["o_done"], m)
                                dve.wait_ge(s["sum_step"], m * 3)
                                dve.tensor_scalar(o_sb[:, qt, bass.ds(h * HD, HD)], ps_o[:, 0:HD], row_inv, None,
                                                  ALU.mult).then_inc(s["o_scaled"], 1)
                        dve.wait_ge(s["ot_done"], na)
                        dve.tensor_copy(o_t[:], ps_t).then_inc(s["ot_copied"], 1)
                        dve.wait_ge(s["wo_done"], na)
                        dve.tensor_tensor(X[:, b, :, :].rearrange("p t d -> p (t d)"), ps_v,
                                          X[:, b, :, :].rearrange("p t d -> p (t d)"), ALU.add).then_inc(s["x_done"], 1)
                    else:
                        nf = b + (FFN[phase] * B + 1)
                        dve.wait_ge(s["xt_copied"], n)
                        dve.tensor_scalar(part_r[:], xt[:, 0:S], mu_rest[:, 0:1], None, ALU.mult)
                        dve.tensor_scalar(part_k[:], xt[:, 0:S], mu_rest[:, 1:2], None, ALU.mult).then_inc(s["mix_step"], 1)
                        dve.wait_ge(s["mix_step"], nf)
                        dve.scalar_tensor_tensor(mix_r[:], xt[:, 1:1 + S], w["mu_r"], part_r[:], ALU.mult, ALU.add)
                        dve.scalar_tensor_tensor(mix_k[:], xt[:, 1:1 + S], w["mu_k"], part_k[:], ALU.mult, ALU.add)\
                           .then_inc(s["mixed"], 1)
                        dve.wait_ge(s["k_done"], nf)
                        dve.tensor_scalar(relu_k[:], ps_k, 0.0, None, ALU.max).then_inc(s["relu_done"], 1)
                        dve.wait_ge(s["relu_done"], nf)
                        dve.tensor_tensor(act_k[:], relu_k[:], relu_k[:], ALU.mult).then_inc(s["k_acted"], 1)
                        dve.wait_ge(s["gate_done"], nf)
                        dve.scalar_tensor_tensor(gated[:], gate[:], 1.0, ps_v, ALU.add, ALU.mult)\
                           .then_inc(s["gated_done"], 1)
                        dve.wait_ge(s["gated_done"], nf)
                        xb = X[:, b, :, :].rearrange("p t d -> p (t d)")
                        dve.scalar_tensor_tensor(xb, gated[:], 0.5, xb, ALU.mult, ALU.add).then_inc(s["x_done"], 1)

        def store(sp, b, signal):
            sp.dma_start(out[b].rearrange("(t p) d -> p t d", p=P), X[:, b, :, :]).then_inc(signal, 16)

        @block.sync
        def _(sp):
            xs = dram["x"].rearrange("b (t p) d -> p b t d", p=P)
            sp.dma_start(packs["first"][:], dram["pack_first"]).then_inc(loaded["first"], 16)
            sp.dma_start(X[:, 0:1, :, :], xs[:, 0:1]).then_inc(x_first, 16)
            sp.dma_start(w_up[:], dram["w_up"]).then_inc(up_loaded, 16)
            sp.dma_start(packs["fold"][:], dram["pack_fold"]).then_inc(loaded["fold"], 16)
            sp.dma_start(X[:, 1:B, :, :], xs[:, 1:B]).then_inc(x_rest, 16)
            sp.dma_start(norm_sum[:], dram["norm_sum"]).then_inc(tables_loaded, 16)
            sp.dma_start(packs["rest"][:], dram["pack_rest"]).then_inc(loaded["rest"], 16)
            sp.wait_ge(stacks_zeroed, 4)

            def stack_half(kind, half, count):
                for v in (QM, KP, QP, KM) if kind == "A" else (KP, QM):
                    sp.wait_ge(parts_done[v], count)
                    for term, part in enumerate(PARTS_OF[v]):
                        rows = slice(HD * term, HD * term + HD)
                        if kind == "B" and v == KP:
                            dst, src = stacks[v][rows, half, 0, :], parts[v][0:57:8, part, :]
                        else:
                            dst, src = stacks[v][rows, half, :, :], parts[v][64 * half:64 * half + 64, part, :]
                        sp.dma_start(dst, src).then_inc(stacked[v][half], 16)

            def job_dmas(job):
                if job.known:
                    sp.wait_ge(scores_done, job.chunk())
                    sp.sem_inc(passed["sync"], 1)
                stack_half(job.kind, 1, job.n(1))
                if job.known < 2 * B - 1:
                    sp.wait_ge(scores_done, job.chunk(job.chunks // 2))
                    sp.sem_inc(passed["sync"], 1)
                    stack_half(pre_kind(job.known), 0, job.n(2))
                if job.known > B:
                    sp.wait_ge(x_done, job.n())
                    store(sp, job.at(1, -1), stored)

            stack_half("A", 0, 1)
            loops(sp, job_dmas)
            sp.wait_ge(aux_emptied, copied(Job("B", None, 1, B - 1), "norms"))
            sp.dma_start(norm_rows[0:1, 0, :], norms[0:32, :]).then_inc(norms_moved, 16)
            sp.dma_start(norm_rows[0:1, 1, :], norms[32:64, :]).then_inc(norms_moved, 16)
            sp.wait_ge(x_done, 2 * B)
            store(sp, B - 1, stored)
            sp.wait_ge(stored, 16 * B)
            general(sp, general_sync)

        def split(eng, v, ready, count, rest_buf, before):
            src, dst = folded[v], parts[v]

            def rounded(to, of):
                if eng is nc.gpsimd:
                    return eng.tensor_tensor(to, of, bass.AP(one, 0, [[1, P], [0, S]]), ALU.mult)
                return eng.tensor_scalar(to, of, 1.0, None, ALU.mult)

            if not isinstance(count, int) or count > 1:
                for half in range(2):
                    eng.wait_ge(stacked[v][half], (count - 1) * (16 * TERMS))
            eng.wait_ge(*ready)
            rounded(dst[:, 0, :], src[:]).then_inc(part_step[v], 1)
            if before is not None:
                eng.wait_ge(parts_done[before[0]], before[1])
            eng.wait_ge(part_step[v], count * 3 - 2)
            eng.tensor_tensor(rest_buf[:], src[:], dst[:, 0, :], ALU.subtract).then_inc(part_step[v], 1)
            eng.wait_ge(part_step[v], count * 3 - 1)
            rounded(dst[:, 1, :], rest_buf[:]).then_inc(part_step[v], 1)
            eng.wait_ge(part_step[v], count * 3)
            eng.tensor_tensor(dst[:, 2, :], rest_buf[:], dst[:, 1, :], ALU.subtract).then_inc(parts_done[v], 1)

        @block.gpsimd
        def _(pool):
            pool.memset(minus_half[:], -0.5).then_inc(pool_consts, 1)
            pool.memset(one[:], 1.0).then_inc(pool_consts, 1)
            for v in range(4):
                pool.memset(stacks[v][:], 0.0).then_inc(stacks_zeroed, 1)
            pool.wait_ge(pool_consts, 2)

            def root(side, count):
                pool.wait_ge(lns[side]["var"], count)
                pool.tensor_tensor(ln[side]["rstd"][:], ln[side]["var_eps"][:], minus_half[:], ALU.pow)\
                    .then_inc(lns[side]["rstd"], 1)

            def square(kind, k_ready, norms_step):
                pool.wait_ge(*k_ready)
                if norms_step is not None:
                    pool.wait_ge(aux_filled, norms_step + 1)
                q = folded[QP if kind == "A" else QM]
                pool.tensor_tensor(squares[:, 0, :], q[:], q[:], ALU.mult)
                pool.tensor_tensor(squares[:, 1, :], folded[KP][:], folded[KP][:], ALU.mult).then_inc(squared, 1)

            def act_square(relu_copied):
                pool.wait_ge(aux_emptied, relu_copied)
                pool.tensor_tensor(act_k[:], relu_k[:], relu_k[:], ALU.mult).then_inc(k_acted, 1)

            def rope_add(v, sin_done):
                other = folded[QP if v == QM else KM]
                pool.wait_ge(aux_emptied, sin_done)
                pool.tensor_tensor(folded[v][:], folded[v][:], other[:], ALU.add).then_inc(roped[v], 1)

            def pool_job(job):
                nxt, n = pre_kind(job.known), job.known
                roped_count = 1 if n == B - 1 else job.at(1, 2)
                if nxt == "A":
                    q_ready, k_ready = (aux_emptied, copied(job, "q")), (aux_emptied, copied(job, "k"))
                    split(pool, QM, q_ready, job.n(2), rest[0], (QP, job.n(1)))
                    split(pool, QP, q_ready, job.n(2), rest[0], (QM, job.n(2)))
                    if n:
                        root("post", job.n())
                    split(pool, KM, k_ready, job.n(2), rest[1], (KP, job.n(2)))
                    square(nxt, k_ready, aux_index(job, "norms"))
                elif nxt == "B":
                    rope_add(KP, copied(job, "k_swapped"))
                    split(pool, KP, (roped[KP], roped_count), job.n(2), rest[1],
                          (KM, B) if n == B - 1 else (KP, job.n(1)))
                    root("post", job.n())
                    rope_add(QM, copied(job, "q_swapped"))
                    split(pool, QM, (roped[QM], roped_count), job.n(2), rest[0],
                          (QP, B) if n == B - 1 else (QM, job.n(1)))
                else:
                    root("post", job.n())
                if n:
                    act_square(copied(job, "ffn_k"))
                if nxt == "B":
                    square(nxt, (roped[KP], roped_count), aux_index(job, "norms"))
                if nxt:
                    root("pre", job.n(3))

            root("pre", 1)
            q_ready = (aux_emptied, AUX_PROLOGUE.index("q") + 1)
            split(pool, QM, q_ready, 1, rest[0], None)
            split(pool, QP, q_ready, 1, rest[0], (QM, 1))
            k_ready = (aux_emptied, AUX_PROLOGUE.index("k") + 1)
            split(pool, KM, k_ready, 1, rest[1], (KP, 1))
            square("A", k_ready, None)
            root("pre", 2)
            loops(pool, pool_job)
            root("post", 2 * B)
            act_square(tail_copied("ffn_k"))
            general(pool, general_pool)

        @block.scalar
        def _(act):
            def copy_o(half, bursts):
                act.wait_ge(products_done, bursts)
                act.activation(o_raw[:, half, :], o_bank[:], ACT.Copy).then_inc(o_copied, 1)

            def step(name, index):
                dst = {"pre_xt": ln["pre"]["xt"][:, 1:1 + S], "post_xt": ln["post"]["xt"][:, 1:1 + S],
                       "o_t": o_t[:], "ffn_r": gate[:]}.get(name)
                if dst is not None:
                    act.wait_ge(aux_filled, index + 1)
                    fn, scale = (ACT.Tanh, 0.5) if name == "ffn_r" else (ACT.Copy, 1.0)
                    act.activation(dst, aux[:], fn, scale=scale).then_inc(aux_emptied, 1)

            def act_job(job):
                scale = SCALE_A if job.kind == "A" else SCALE_B
                steps = aux_steps(job.known)

                def exps(u, chunks):
                    for c in chunks:
                        k = chunk_in_job(job.kind, u, c)
                        slot = slots[job.slot_of(k)]
                        act.wait_ge(diag_done, job.chunk(k + 1))
                        if job.kind == "A":
                            dst, src = probs[:, u % 2, c, :], slot
                        elif u % 2 == 0:
                            dst, src = probs[:, 0, c, 0:896], slot[:, 0:896]
                        else:
                            dst = probs[:, 1, 2 * c:2 * c + 2, 0:384]
                            src = slot.rearrange("p (h q) -> p h q", h=2)[:, :, 0:384]
                        act.activation(dst, src, ACT.Exp, scale=scale).then_inc(exp_done, 1)

                def steps_at(u, where):
                    for su, place, name in steps:
                        if (su, place) == (u, where):
                            step(name, aux_index(job, name))

                for u in range(8):
                    first, second = slot_groups(job.kind, u)
                    steps_at(u, "a")
                    exps(u, first[:2])
                    steps_at(u, "b")
                    exps(u, first[2:])
                    if u == 0 and job.known:
                        copy_o(1, job.burst())
                    if u == 4:
                        copy_o(0, job.burst(4))
                    exps(u, second)

            step("pre_xt", AUX_PROLOGUE.index("pre_xt"))
            loops(act, act_job)
            copy_o(1, 16 * B)
            for k, name in enumerate(AUX_TAIL):
                step(name, aux_before(2 * B) + k)
            general(act, general_act)

        @block.tensor
        def _(pe):
            ident = w["identity"]
            def claim(index):
                if not isinstance(index, int) or index > 0:
                    pe.wait_ge(aux_emptied, index)

            def tiles_of(fn):
                for t in range(TILES):
                    last = fn(t, slice(t * P, (t + 1) * P))
                last.then_inc(aux_filled, 1)

            def step(name, kind, index, pre, post, o_count):
                claim(index)
                if name in ("pre_xt", "post_xt"):
                    side, count = ("pre", pre) if name == "pre_xt" else ("post", post)
                    pe.wait_ge(lns[side]["normed"], count)
                    tiles_of(lambda t, c: pe.transpose(aux[:, c], ln[side]["normed"][:, t, :], ident))
                elif name in ("q", "k", "q_swapped", "k_swapped"):
                    weight = {"qA": w["wq_a"], "kA": w_kk[:], "qB": w["wq_b"], "kB": w["wk_b"],
                              "q_swappedB": w["wq_b_swapped"], "k_swappedB": w["wk_b_swapped"]}[name + kind]
                    pe.matmul(aux[:], weight, ln["pre"]["xt"][:, 1:1 + S], start=True, stop=True).then_inc(aux_filled, 1)
                elif name == "v":
                    wv, nv = (w_vv[:], P) if kind == "A" else (w["wv_b"], HD)
                    tiles_of(lambda t, c: pe.matmul(aux[:, t * P:t * P + nv], ln["pre"]["xt"][:, 1 + t * P:1 + (t + 1) * P],
                                                    wv, start=True, stop=True))
                elif name == "norms":
                    pe.wait_ge(squared, o_count)
                    pe.matmul(aux[0:32, :], norm_sum[:], squares[:, 0, :], start=True, stop=True)
                    pe.matmul(aux[32:64, :], norm_sum[:], squares[:, 1, :], start=True, stop=True).then_inc(aux_filled, 1)
                elif name in ("o_first", "o_second"):
                    half = int(name == "o_second")
                    pe.wait_ge(o_copied, o_count)
                    tiles_of(lambda t, c: pe.transpose(aux[:, c], o_raw[:, half, c], ident))
                elif name == "o_t":
                    tiles_of(lambda t, c: pe.transpose(aux[:, c], o_tok[:, t, :], ident))
                elif name == "wo":
                    tiles_of(lambda t, c: pe.matmul(aux[:, c], o_t[:, c], w["wo_a" if kind == "A" else "wo_b"],
                                                    start=True, stop=True))
                elif name == "ffn_k":
                    pe.wait_ge(mixed_k, post)
                    pe.matmul(aux[:], w["w_k"], mix_k[:], start=True, stop=True).then_inc(aux_filled, 1)
                elif name == "ffn_r":
                    pe.wait_ge(mixed_r, post)
                    tiles_of(lambda t, c: pe.matmul(aux[:, c], mix_r[:, c], w["w_r"], start=True, stop=True))
                elif name == "ffn_v":
                    pe.wait_ge(k_acted, post)
                    tiles_of(lambda t, c: pe.matmul(aux[:, c], act_k[:, c], w["w_v"], start=True, stop=True))

            def scores(job, u, c):
                half, second = u // 4, u // 2 % 2
                k = chunk_in_job(job.kind, u, c)
                slot = slots[job.slot_of(k)]
                if k or job.known:
                    if job.known or k >= 3:
                        pe.wait_ge(exp_done, job.chunk(k - 2))
                if c == 0 and u % 4 == 0:
                    for v in (QM, KP, QP, KM) if job.kind == "A" else (QM, KP):
                        pe.wait_ge(stacked[v][half], job.n(1) * (16 * TERMS))
                if job.kind == "A":
                    head = 2 * c + second
                    for i in range(2):
                        kt = 2 * (u % 2) + i
                        keys, edge = slice(kt * P, (kt + 1) * P), kt * P
                        bank = slot[:, i * S:(i + 1) * S]
                        if kt:
                            last = pe.matmul(bank[:, 0:edge], stacks[KM][:, half, head, keys],
                                             stacks[QP][:, half, head, 0:edge], start=True, stop=True)
                        last = pe.matmul(bank[:, edge:S], stacks[KP][:, half, head, keys],
                                         stacks[QM][:, half, head, edge:S], start=True, stop=True)
                else:
                    if u % 2 == 0:
                        rows = [(0, 2 * c + second, 0), (1, 2 * c + second, S)]
                    else:
                        rows = [(kt, 2 * (2 * c + i) + second, i * S + (kt - 2) * 2 * P)
                                for i in range(2) for kt in (2, 3)]
                    for kt, head, col in rows:
                        last = pe.matmul(slot[:, col:col + S - kt * P], stacks[KP][:, half, 0, kt * P:(kt + 1) * P],
                                         stacks[QM][:, half, head, kt * P:S], start=True, stop=True)
                last.then_inc(scores_done, 1)

            def products(kind, u, exp_count, job_count):
                half, second, pair = u // 4, u // 2 % 2, u % 2
                pe.wait_ge(exp_done, exp_count)
                if u % 4 == 0:
                    pe.wait_ge(v_placed[half], job_count)
                    if half or not isinstance(job_count, int) or job_count > 1:
                        pe.wait_ge(o_copied, job_count * 2 - 2 + half)
                for i in range(2):
                    kt = 2 * pair + i
                    q0, col = (0, i * S) if kind == "A" else (kt * P, i * (2 * P if pair else S))
                    for g in range(GROUPS):
                        last = pe.matmul(o_bank[32 * g:32 * g + 32, q0:S], v_heads[:, half, kt, 2 * g + second, :],
                                         probs[:, u % 2, g, col:col + S - q0],
                                         start=(u % 4 == 0 and i == 0), stop=(u % 4 == 3 and i == 1))
                last.then_inc(products_done, 1)

            def pe_job(job):
                steps = aux_steps(job.known)

                def aux_at(u, place):
                    for su, sp_, name in steps:
                        if (su, sp_) == (u, place):
                            kind = pre_kind(job.known) if name in ("q", "k", "v", "q_swapped", "k_swapped") else \
                                "A" if job.known <= B else "B"
                            o_count = {"norms": job.n(1), "o_first": job.at(2, (0 if job.kind == "A" else 2 * B) + 1),
                                       "o_second": job.at(2, 0 if job.kind == "A" else 2 * B)}.get(name)
                            step(name, kind, aux_index(job, name), job.n(2), job.n(), o_count)

                for u in range(8):
                    first, second = slot_groups(job.kind, u)
                    aux_at(u, "a")
                    for c in first:
                        scores(job, u, c)
                    aux_at(u, "b")
                    if u:
                        products(job.kind, u - 1, job.chunk(chunk_in_job(job.kind, u, 0)), job.n(1))
                    elif job.known:
                        products("A" if job.known <= B else "B", 7, job.chunk(), job.n())
                    for c in second:
                        scores(job, u, c)

            pe.wait_ge(loaded["first"], 16)
            pe.wait_ge(w_summed, 1)
            pe.transpose(aux[:, 0:P], w_sum[:], ident).then_inc(aux_filled, 1)
            claim(1)
            pe.matmul(aux[0:LAT, 0:P], w["w_down"], w_sum_t[:], start=True, stop=True).then_inc(aux_filled, 1)
            claim(2)
            pe.wait_ge(up_loaded, 16)
            pe.matmul(aux[:, 0:P], w_lat_t[:], w_up[:, UP_K, :], start=True, stop=True).then_inc(aux_filled, 1)
            claim(3)
            pe.matmul(aux[:, 0:P], w_lat_t[:], w_up[:, UP_V, :], start=True, stop=True).then_inc(aux_filled, 1)
            for k, name in enumerate(AUX_PROLOGUE[4:]):
                step(name, "A", 4 + k, 1, None, None)
            pe.wait_ge(tables_loaded, 16)
            pe.wait_ge(loaded["rest"], 16)
            loops(pe, pe_job)
            products("B", 7, 56 * B, 2 * B)
            for k, name in enumerate(AUX_TAIL):
                step(name, "B", aux_before(2 * B) + k, None, 2 * B, 4 * B)
            general(pe, general_pe)

        def flat_ap(tensor, offset, *dims):
            width = int(np.prod(tensor.shape[1:]))
            return bass.AP(tensor, offset, [[width, P], *[list(d) for d in dims]])

        def table_ap(name, *repeats):
            at = 0
            for member, cols in PACK_REST:
                if member == name:
                    break
                at += cols
            return flat_ap(packs["rest"], at, *[(0, r) for r in repeats], (1, P))

        @block.vector
        def _(dve):
            def filled(index):
                dve.wait_ge(aux_filled, index + 1)

            def diagonal(job, u, c):
                k = chunk_in_job(job.kind, u, c)
                at = 1024 * job.slot_of(k)
                if job.kind == "A":
                    blocks = flat_ap(psum, at + 256 * (u % 2), (S + P, 2), (1, P))
                    table, op = table_ap("diag_decay", 2), ALU.mult
                elif u % 2 == 0:
                    blocks = flat_ap(psum, at, (S, 2), (1, P))
                    table, op = table_ap("diag_causal", 2), ALU.min
                else:
                    blocks = flat_ap(psum, at, (S, 2), (2 * P, 2), (1, P))
                    table, op = table_ap("diag_causal", 2, 2), ALU.min
                dve.wait_ge(scores_done, job.chunk(k + 1))
                dve.tensor_tensor(blocks, blocks, table, op).then_inc(diag_done, 1)

            def ln_stats(side, b, count):
                t_, s_ = ln[side], lns[side]
                for t in range(TILES):
                    last = dve.bn_stats(t_["stats"][:, t, :], X[:, b, t, :])
                last.then_inc(s_["stats"], 1)
                even, odd = t_["stats"][:, :, 1], t_["stats"][:, :, 4]
                dve.wait_ge(s_["stats"], count)
                dve.tensor_tensor(t_["mean_sum"][:], even, odd, ALU.add)
                dve.tensor_tensor(t_["mean_dif"][:], even, odd, ALU.subtract)
                dve.tensor_tensor(t_["m2_sum"][:], t_["stats"][:, :, 2], t_["stats"][:, :, 5], ALU.add).then_inc(s_["parts"], 1)
                dve.wait_ge(s_["parts"], count)
                dve.tensor_scalar(t_["mean"][:], t_["mean_sum"][:], 0.5, None, ALU.mult)
                dve.tensor_tensor(t_["dif_sq"][:], t_["mean_dif"][:], t_["mean_dif"][:], ALU.mult).then_inc(s_["squares"], 1)
                dve.wait_ge(s_["squares"], count)
                dve.scalar_tensor_tensor(t_["var_p"][:], t_["dif_sq"][:], P / 4, t_["m2_sum"][:], ALU.mult, ALU.add)\
                   .then_inc(s_["var_sum"], 1)
                dve.wait_ge(s_["var_sum"], count)
                dve.tensor_scalar(t_["var_eps"][:], t_["var_p"][:], 1 / P, EPS, ALU.mult, ALU.add).then_inc(s_["var"], 1)

            def ln_normalise(side, b, count):
                t_, s_ = ln[side], lns[side]
                dve.wait_ge(s_["rstd"], count)
                for t in range(TILES):
                    last = dve.tensor_scalar(t_["normed"][:, t, :], X[:, b, t, :], t_["mean"][:, t:t + 1],
                                             t_["rstd"][:, t:t + 1], ALU.subtract, ALU.mult)
                last.then_inc(s_["normed"], 1)

            def folded_free(variants, count):
                if not isinstance(count, int) or count > 1:
                    for v in variants:
                        dve.wait_ge(parts_done[v], count - 1)
                    dve.wait_ge(squared, count - 1)

            def fold(variants, index, count):
                folded_free(variants, count)
                filled(index)
                for v in variants:
                    table = w["fold_down" if v in (QM, KM) else "fold_up"]
                    last = dve.tensor_tensor(folded[v][:], aux[:], table, ALU.mult)
                last.then_inc(aux_emptied, 1)

            def rope_cos(v, index, count):
                folded_free([v], count)
                filled(index)
                dve.tensor_tensor(folded[v][:], aux[:], w["rope_cos"], ALU.mult).then_inc(aux_emptied, 1)

            def rope_sin(v, index, first):
                other = folded[QP if v == QM else KM]
                if first:
                    dve.wait_ge(parts_done[QP if v == QM else KM], B)
                filled(index)
                dve.tensor_tensor(other[:], aux[:], w["rope_sin"], ALU.mult).then_inc(aux_emptied, 1)

            def stage_v(kind, index, count):
                if not isinstance(count, int) or count > 1:
                    for half in range(2):
                        dve.wait_ge(v_placed[half], count - 1)
                filled(index)
                nv = P if kind == "A" else HD
                dve.tensor_copy(v_stage[:, :, 0:nv], aux[:].rearrange("p (t d) -> p t d", d=P)[:, :, 0:nv])\
                   .then_inc(aux_emptied, 1)

            def place_v(kind, half, staged, bursts):
                if not isinstance(bursts, int) or bursts > 0:
                    dve.wait_ge(products_done, bursts)
                dve.wait_ge(aux_emptied, staged)
                for second in range(2):
                    if kind == "A":
                        src = flat_ap(v_stage, 64 * half + HD * second, (P, TILES), (2 * HD, GROUPS), (1, HD))
                    else:
                        src = flat_ap(v_stage, 0, (P, TILES), (0, GROUPS), (1, HD))
                    dst = v_heads[:, half, :, second::2, HD * second:HD * second + HD]
                    last = dve.tensor_copy(dst, src)
                last.then_inc(v_placed[half], 1)

            def normalise_o(half, index, count):
                cols = aux[:].rearrange("p (g c) -> p g c", c=32)
                filled(index)
                dve.reciprocal(inv_sum[:], cols[:, :, 2 * HD:2 * HD + 2]).then_inc(inv_done, 1)
                dve.wait_ge(inv_done, count)
                for second in range(2):
                    dst = flat_ap(o_tok, 64 * half + HD * second, (P, TILES), (2 * HD, GROUPS), (1, HD))
                    src = flat_ap(aux, HD * second, (P, TILES), (32, GROUPS), (1, HD))
                    inv = flat_ap(inv_sum, second, (2 * GROUPS, TILES), (2, GROUPS), (0, HD))
                    last = dve.tensor_tensor(dst, src, inv, ALU.mult)
                last.then_inc(aux_emptied, 1)

            def add_attention(b, index):
                filled(index)
                dve.tensor_tensor(xb(b), aux[:], xb(b), ALU.add).then_inc(aux_emptied, 1)
                dve.wait_ge(aux_emptied, index + 1)
                dve.sem_inc(passed["vector"], 1)

            def mix(which, xt_copied, count):
                dst, part, mu, scaled, signal = ((mix_k, part_k, "mu_k", prev_scaled_k, mixed_k),
                                                 (mix_r, part_r, "mu_r", prev_scaled_r, mixed_r))[which]
                rest_of = mu_rest[:, 1 - which:2 - which]
                dve.wait_ge(aux_emptied, xt_copied)
                dve.tensor_scalar(part[:], ln["post"]["xt"][:, 0:S], rest_of, None, ALU.mult).then_inc(scaled, 1)
                dve.wait_ge(scaled, count)
                dve.scalar_tensor_tensor(dst[:], ln["post"]["xt"][:, 1:1 + S], w[mu], part[:], ALU.mult, ALU.add)\
                   .then_inc(signal, 1)

            def relu(index):
                filled(index)
                dve.tensor_scalar(relu_k[:], aux[:], 0.0, None, ALU.max).then_inc(aux_emptied, 1)

            def add_ffn(b, index):
                filled(index)
                dve.scalar_tensor_tensor(gated[:], gate[:], 1.0, aux[:], ALU.add, ALU.mult).then_inc(aux_emptied, 1)
                dve.wait_ge(aux_emptied, index + 1)
                dve.scalar_tensor_tensor(xb(b), gated[:], 0.5, xb(b), ALU.mult, ALU.add).then_inc(x_done, 1)

            def side_work(job, u, place):
                n, nxt, idx = job.known, pre_kind(job.known), lambda name: aux_index(job, name)
                prev_b = job.at(1, -1) if n != B else B - 1
                next_b = job.at(1, 1) if n != B - 1 else 0
                at = (u, place)
                if at == (0, "early"):
                    filled(idx("norms"))
                    dve.reduce_max(norms[:, bass.ds(job.n(), 1)], aux[0:64, :], AX.X).then_inc(aux_emptied, 1)
                if at == (0, "mid") and nxt:
                    ln_normalise("pre", next_b, job.n(2))
                if at == (1, "late"):
                    if nxt == "A":
                        fold((KP, KM), idx("k"), job.n(2))
                    if nxt == "B":
                        rope_sin(KP, idx("k_swapped"), n == B - 1)
                    staged = AUX_PROLOGUE.index("v") + 1 if n == 0 else copied_before(job, "v")
                    place_v(job.kind, 1, staged, job.burst())
                if at == (2, "early") and n:
                    normalise_o(1, idx("o_second"), job.n() * 2)
                if at == (6, "late") and nxt:
                    place_v(nxt, 0, copied(job, "v"), job.burst(4))
                if at == ((7, "mid") if nxt == "A" else (6, "late")) and nxt:
                    if n > 1:
                        dve.wait_ge(x_done, job.n(-1))
                    ln_stats("pre", (n + 2) % B if job.it is None else job.at(1, 2) % B, job.n(3))
                if nxt == "A":
                    if at == (1, "early"):
                        fold((QM, QP), idx("q"), job.n(2))
                    if at == (2, "late"):
                        split(dve, KP, (aux_emptied, copied(job, "k")), job.n(2), rest[1], (KM, job.n(1)))
                    if at == (3, "early") and n:
                        add_attention(prev_b, idx("wo"))
                    if at == (3, "late"):
                        if n:
                            ln_stats("post", prev_b, job.n())
                        stage_v("A", idx("v"), job.n(2))
                    if at == (4, "mid") and n:
                        ln_normalise("post", prev_b, job.n())
                    if at == (4, "late") and n:
                        mix(0, copied(job, "post_xt"), job.n())
                    if at == (5, "early"):
                        normalise_o(0, idx("o_first"), job.n() * 2 + 1)
                    if at == (5, "late") and n:
                        mix(1, copied(job, "post_xt"), job.n())
                        relu(idx("ffn_k"))
                    if at == (6, "late") and n:
                        add_ffn(prev_b, idx("ffn_v"))
                    return
                if nxt and at == (1, "early"):
                    rope_cos(KP, idx("k"), job.n(2))
                if nxt and at == (3, "early"):
                    rope_cos(QM, idx("q"), job.n(2))
                if at == (3, "late"):
                    add_attention(prev_b, idx("wo"))
                    ln_stats("post", prev_b, job.n())
                if nxt and at == (4, "early"):
                    rope_sin(QM, idx("q_swapped"), n == B - 1)
                if at == (4, "late"):
                    if nxt:
                        stage_v("B", idx("v"), job.n(2))
                    ln_normalise("post", prev_b, job.n())
                if at == (5, "mid"):
                    mix(0, copied(job, "post_xt"), job.n())
                if at == (5, "late"):
                    normalise_o(0, idx("o_first"), job.n() * 2 + 1)
                    mix(1, copied(job, "post_xt"), job.n())
                if at == (6, "early"):
                    relu(idx("ffn_k"))
                if at == (7, "early"):
                    add_ffn(prev_b, idx("ffn_v"))

            def copied_before(job, name):
                n = job.known - 1
                k = [s[2] for s in aux_steps(n)].index(name)
                back = len(aux_steps(n)) - k
                return aux_before(job.known) - back + 1 if job.it is None else job.aux(1 - back)

            def dve_job(job):
                for u in range(8):
                    first, second = slot_groups(job.kind, u)
                    side_work(job, u, "early")
                    for c in first[:-1]:
                        diagonal(job, u, c)
                    side_work(job, u, "mid")
                    diagonal(job, u, first[-1])
                    side_work(job, u, "late")
                    for c in second:
                        diagonal(job, u, c)

            dve.memset(ln["post"]["xt"][:, 0:1], 0.0).then_inc(dve_consts, 1)
            dve.memset(v_heads[:], 0.0).then_inc(dve_consts, 1)
            dve.wait_ge(dve_consts, 2)
            for second in range(2):
                dve.memset(v_heads[:, :, :, second::2, 2 * HD + second:2 * HD + second + 1], 1.0).then_inc(dve_consts, 1)
            dve.wait_ge(loaded["first"], 16)
            dve.tensor_tensor(w_sum[:], w["wk_a"], w["wv_a"], ALU.add).then_inc(w_summed, 1)
            dve.wait_ge(x_first, 16)
            ln_stats("pre", 0, 1)
            for index, (dst, src) in enumerate(((w_sum_t[:], aux[:, 0:P]), (w_lat_t[:], aux[0:LAT, 0:P]),
                                                (w_kk[:], aux[:, 0:P]), (w_vv[:], aux[:, 0:P]))):
                filled(index)
                dve.tensor_copy(dst, src).then_inc(aux_emptied, 1)
            ln_normalise("pre", 0, 1)
            dve.wait_ge(loaded["fold"], 16)
            fold((QM, QP), AUX_PROLOGUE.index("q"), 1)
            fold((KP, KM), AUX_PROLOGUE.index("k"), 1)
            k_ready = (aux_emptied, AUX_PROLOGUE.index("k") + 1)
            split(dve, KP, k_ready, 1, rest[1], None)
            dve.wait_ge(dve_consts, 4)
            stage_v("A", AUX_PROLOGUE.index("v"), 1)
            place_v("A", 0, AUX_PROLOGUE.index("v") + 1, 0)
            dve.wait_ge(loaded["rest"], 16)
            for i, mu in enumerate(("mu_r", "mu_k")):
                dve.tensor_scalar(mu_rest[:, i:i + 1], w[mu], -1.0, 1.0, ALU.mult, ALU.add).then_inc(mu_ready, 1)
            dve.wait_ge(x_rest, 16)
            ln_stats("pre", 1, 2)
            dve.wait_ge(mu_ready, 2)
            loops(dve, dve_job)
            b = B - 1
            at = {name: aux_before(2 * B) + k for k, name in enumerate(AUX_TAIL)}
            normalise_o(1, at["o_second"], 4 * B)
            add_attention(b, at["wo"])
            ln_stats("post", b, 2 * B)
            ln_normalise("post", b, 2 * B)
            mix(0, at["post_xt"] + 1, 2 * B)
            mix(1, at["post_xt"] + 1, 2 * B)
            relu(at["ffn_k"])
            add_ffn(b, at["ffn_v"])
            for kind, scale in ((0, SCALE_A), (1, SCALE_B)):
                dve.memset(norm_rows[0:1, 2, :].rearrange("p (r k b) -> p r k b", k=2, b=B)[:, :, kind, :],
                           float(scale * scale / (LIMIT * LIMIT))).then_inc(bound_step, 1)
            dve.wait_ge(norms_moved, 32)
            for by in (1, 2):
                dve.tensor_tensor(norm_rows[0:1, 0, :], norm_rows[0:1, 0, :], norm_rows[0:1, by, :], ALU.mult)\
                   .then_inc(bound_step, 1)
                dve.wait_ge(bound_step, 2 + by)
            dve.tensor_scalar(norm_rows[0:1, 1, :], norm_rows[0:1, 0, :], 1.0, 0.0, ALU.is_lt, ALU.is_equal)\
               .then_inc(bound_step, 1)
            dve.wait_ge(bound_step, 5)
            dve.reduce_max(flag_f[:], norm_rows[0:1, 1, :], AX.X).then_inc(bound_step, 1)
            dve.wait_ge(bound_step, 6)
            dve.tensor_copy(flag[:], flag_f[:]).then_inc(flag_done, 1)
            general(dve, general_dve)


def tables():
    i = np.arange(S, dtype=np.float32)
    dist = np.abs(i[:, None] - i[None, :])
    decay = np.exp(np.float32(-DECAY) * dist).astype(np.float32)
    causal = np.where(i[:, None] >= i[None, :], np.float32(3.0e38), np.float32(-3.0e38)).astype(np.float32)
    freqs = (np.float32(1.0) / np.float32(1000.0) ** (np.arange(0, HD, 2, dtype=np.float32) / np.float32(HD)))
    ang = i[None, :] * freqs[:, None].astype(np.float32)
    cos, sin = np.cos(ang), np.sin(ang)
    row_d, row_head = row_order()
    k, q = np.arange(P)[:, None].astype(np.float64), np.arange(P)[None, :]
    along = np.arange(S, dtype=np.float64)
    by_tile = lambda m: np.ascontiguousarray(m.reshape(TILES, P, S).transpose(1, 0, 2))
    heads = (row_head[:, None] == np.arange(H)[None, :]).astype(np.float32)
    return {
        "identity": np.eye(P, dtype=np.float32),
        "head_mask": heads,
        "norm_sum": np.concatenate([heads, 0 * heads], axis=1),
        "decay": by_tile(decay),
        "causal": by_tile(causal),
        "rope_cos": np.concatenate([cos, cos])[row_d].astype(np.float32),
        "rope_sin": np.concatenate([-sin, sin])[row_d].astype(np.float32),
        "fold_down": np.tile(np.exp(-DECAY * along), (P, 1)).astype(np.float32),
        "fold_up": np.tile(np.exp(DECAY * along), (P, 1)).astype(np.float32),
        "diag_decay": np.exp(-DECAY * (np.abs(q - k) - (q - k))).astype(np.float32),
        "diag_causal": np.where(q >= k, np.float32(3.0e38), np.float32(-3.0e4)).astype(np.float32),
    }


def row_order():
    rows = np.arange(P)
    return rows // HALF % HD, rows // 64 * HALF + rows % HALF


def kernel(**inputs):
    import concourse.bacc as bacc
    from concourse.bass_utils import run_bass_kernel_spmd

    x = {k.removeprefix("L0_"): np.ascontiguousarray(v) for k, v in inputs.items()}
    row_d, row_head = row_order()
    cols = row_head * HD + row_d
    split = np.array([*range(0, HD, 2), *range(1, HD, 2)])
    swap = np.array([*range(1, HD, 2), *range(0, HD, 2)])
    wq_b = x["attn_b_wq"].T
    arrays = {
        "wq_a": x["attn_a_Wq"][:, cols], "wk_a": x["attn_a_Wk"], "wv_a": x["attn_a_Wv"],
        "wo_a": x["attn_a_Wo"], "w_down": x["attn_a_W_down_kv"],
        "wq_b": wq_b[:, row_head * HD + split[row_d]], "wq_b_swapped": wq_b[:, row_head * HD + swap[row_d]],
        "wk_b": x["attn_b_wk"][:, split[row_d]], "wk_b_swapped": x["attn_b_wk"][:, swap[row_d]],
        "wv_b": x["attn_b_wv"], "wo_b": x["attn_b_wo"].T,
        "w_r": x["ffn_W_r"].T, "w_k": x["ffn_W_k"].T, "w_v": x["ffn_W_v"].T,
        "mu_r": x["ffn_mu_r"].reshape(P, 1), "mu_k": x["ffn_mu_k"].reshape(P, 1),
        **tables(),
    }
    fed = {"x": x["attn_a_x"], "decay": arrays["decay"], "causal": arrays["causal"],
           "w_up": np.stack([x["attn_a_W_up_k"][:, cols], x["attn_a_W_up_v"]], axis=1),
           "norm_sum": arrays["norm_sum"].astype(mybir.dt.np(BF16))}
    for pack, members in PACKS.items():
        fed["pack_" + pack] = np.concatenate([arrays[name] for name, _ in members], axis=1)
    fed = {k: np.ascontiguousarray(v) for k, v in fed.items()}
    nc = bacc.Bacc("TRN2", target_bir_lowering=False, num_devices=1)
    dram = {k: nc.dram_tensor(k + "_dram", v.shape, mybir.dt.from_np(v.dtype), kind="ExternalInput").ap()
            for k, v in fed.items()}
    out = nc.dram_tensor("out_0_dram", (B, S, P), F32, kind="ExternalOutput").ap()
    build(nc, dram, out)
    result = run_bass_kernel_spmd(nc, [{k + "_dram": v for k, v in fed.items()}], core_ids=[0])
    return result.results[0]["out_0_dram"]
```

```python
import numpy as np
import concourse.bass as bass
import concourse.mybir as mybir
from contextlib import ExitStack

F32 = mybir.dt.float32
BF16 = mybir.dt.bfloat16
I32 = mybir.dt.int32
ALU = mybir.AluOpType
ACT = mybir.ActivationFunctionType
AX = mybir.AxisListType

P = 128
B, S = 8, 512
TILES = S // P
H, HD = 16, 8
LAT = 32
HALF = H // 2
GROUPS = 4
CLAMP = 10000.0
EPS = 1e-5
DECAY = 0.01 * 0.01
LIMIT = 60.0
SCALE_A = float(np.float32(1.0) / (np.sqrt(np.float32(P)) + np.float32(1e-8)))
SCALE_B = float(np.float32(1.0) / np.float32(np.sqrt(HD)))

Q_PARTS = (0, 0, 0, 1, 1, 2)
K_PARTS = (0, 1, 2, 0, 1, 0)
TERMS = len(Q_PARTS)
STACK = 72
QM, QP, KP, KM = range(4)
PARTS_OF = {QM: Q_PARTS, QP: Q_PARTS, KP: K_PARTS, KM: K_PARTS}

UP_K, UP_V = 0, 1
PACK_FIRST = [("identity", P), ("wk_a", P), ("wv_a", P), ("w_down", LAT), ("wq_a", P)]
PACK_FOLD = [("fold_down", S), ("fold_up", S)]
PACK_REST = [("wo_a", P), ("wq_b", P), ("wq_b_swapped", P), ("wk_b", P), ("wk_b_swapped", P),
             ("wk_b_pair", P), ("wv_b", HD),
             ("wo_b", P), ("w_r", P), ("w_k", P), ("w_v", P), ("mu_r", 1), ("mu_k", 1),
             ("diag_decay", P), ("diag_causal", P), ("head_mask", H), ("rope_cos", S), ("rope_sin", S)]
PACKS = {"first": PACK_FIRST, "fold": PACK_FOLD, "rest": PACK_REST}


class Job:

    def __init__(self, kind, it, step, first):
        self.kind, self.it, self.step, self.first = kind, it, step, first
        self.chunks = 32 if kind == "A" else 24

    def at(self, per, base):
        fixed = self.first * per + base
        return fixed if self.it is None else self.it * (self.step * per) + fixed

    def n(self, more=0):
        return self.at(1, (0 if self.kind == "A" else B) + more)

    def burst(self, more=0):
        return self.at(8, (0 if self.kind == "A" else 8 * B) + more)

    def chunk(self, more=0):
        return self.at(self.chunks, (0 if self.kind == "A" else 32 * B) + more)

    def aux(self, more=0):
        return self.at(AUX_PER_JOB[self.kind], AUX_BASE[self.kind] + more)

    @property
    def known(self):
        return self.first + (0 if self.kind == "A" else B)

    def slot_of(self, c):
        return (self.first * self.chunks + (0 if self.kind == "A" else 32 * B) + c) % 3


def pre_kind(n):
    return None if n == 2 * B - 1 else "A" if n < B - 1 else "B"


def aux_steps(n):
    nxt = pre_kind(n)
    if nxt == "A":
        steps = [(0, "a", "norms"), (0, "b", "pre_xt"), (1, "a", "q"), (1, "b", "k"), (4, "a", "v"),
                 (5, "b", "o_first")]
        post = [(2, "a", "o_second"), (2, "b", "o_t"), (3, "a", "wo"), (5, "a", "post_xt"),
                (6, "a", "ffn_k"), (6, "b", "ffn_r"), (7, "a", "ffn_v")]
    else:
        steps = [(0, "a", "norms"), (7, "b", "o_first")]
        post = [(2, "a", "o_second"), (2, "b", "o_t"), (3, "b", "wo"), (5, "a", "post_xt"),
                (6, "a", "ffn_k"), (6, "b", "ffn_r"), (7, "a", "ffn_v")]
    if nxt == "B":
        steps += [(0, "b", "pre_xt"), (1, "a", "q"), (1, "b", "k"), (3, "a", "q_swapped"), (4, "a", "v")]
    return sorted(steps + (post if n else []))


AUX_PROLOGUE = ["w_sum_t", "w_lat_t", "pre_xt", "q", "w_kk", "w_vv", "k", "v"]
AUX_TAIL = ["o_second", "o_t", "wo", "post_xt", "ffn_k", "ffn_r", "ffn_v"]


def aux_before(n):
    return len(AUX_PROLOGUE) + sum(len(aux_steps(m)) for m in range(n))


GENERAL_SEMS = """x_loaded tables_loaded stats_done parts_done squares_done var_sum_done var_done rstd_done normed_done
    xt_done xt_copied proj_done rot_step proj_copied head_picked scores_done w_step weighted sum_step max_done
    exp_done pt_done pt_copied o_done o_scaled ot_done ot_copied wo_done x_done mix_step mixed k_done relu_done
    k_acted ffn_done gate_done gated_done stored""".split()

AUX_PER_JOB = {"A": len(aux_steps(1)), "B": len(aux_steps(B + 1))}
AUX_BASE = {"A": aux_before(1) - AUX_PER_JOB["A"], "B": aux_before(B)}


def aux_index(job, name):
    k = [s[2] for s in aux_steps(job.known)].index(name)
    return aux_before(0) + k if job.known == 0 else job.aux(k)


def build(nc, dram, out):
    with ExitStack() as ctx:
        def sb(name, shape, dt=F32):
            return ctx.enter_context(nc.sbuf_tensor(name, shape, dt))

        def sem(name):
            return ctx.enter_context(nc.semaphore(name))

        X = sb("residual", [P, B, TILES, P])
        packs, w = {}, {}
        for pack, members in PACKS.items():
            packs[pack] = sb("pack_" + pack, [P, sum(c for _, c in members)])
            at = 0
            for name, cols in members:
                w[name] = packs[pack][:, at:at + cols]
                at += cols
        w_up = sb("w_up", [LAT, 2, P])
        norm_sum = sb("norm_sum", [P, 2, 32], BF16)
        w_sum = sb("w_sum", [P, P])
        w_sum_t = sb("w_sum_t", [P, P])
        w_lat_t = sb("w_lat_t", [LAT, P])
        w_kk = sb("w_kk", [P, P])
        w_vv = sb("w_vv", [P, P])
        w_v_half = sb("w_v_half", [P, P])
        mu_rest = sb("mu_rest", [P, 2])
        minus_half = sb("minus_half", [P, TILES])
        one = sb("one", [P, 1])

        ln_names = "mean_sum mean_dif m2_sum mean dif_sq var_p var_eps rstd".split()
        ln = {side: {n: sb(f"{side}_{n}", [P, TILES]) for n in ln_names} for side in ("pre", "post")}
        for side in ("pre", "post"):
            ln[side]["stats"] = sb(side + "_stats", [P, TILES, 6])
            ln[side]["normed"] = sb(side + "_normed", [P, TILES, P])
            ln[side]["xt"] = sb(side + "_xt", [P, 1 + S])

        folded = [sb(f"folded_{v}", [P, S]) for v in range(4)]
        rest = [sb(f"rest_{v}", [P, S]) for v in range(2)]
        parts = [sb(f"parts_{v}", [P, 3, S], BF16) for v in range(4)]
        stacks = [sb(f"stack_{v}", [STACK, 2, HALF, S], BF16) for v in range(4)]
        squares = sb("squares", [P, 2, S], BF16)
        norms = sb("norms", [64, 2 * B])
        v_stage = sb("v_stage", [P, TILES, P])
        v_heads = sb("v_heads", [P, 2, TILES, HALF, 32])
        probs = sb("probs", [P, 2, GROUPS, 2 * S])
        o_raw = sb("o_raw", [P, 2, S])
        inv_sum = sb("inv_sum", [P, TILES * GROUPS, 2])
        o_tok = sb("o_tok", [P, TILES, P])
        o_t = sb("o_t", [P, S])
        part_r, part_k, mix_r, mix_k, relu_k, act_k, gate, gated = [
            sb(n, [P, S]) for n in "part_r part_k mix_r mix_k relu_k act_k gate gated".split()]
        norm_rows = sb("norm_rows", [1, 3, 32 * 2 * B])
        flag_f = sb("flag_f", [1, 1])
        flag = sb("flag", [1, 1], I32)

        psum = ctx.enter_context(nc.psum_tensor("scores", [P, 3 * 1024], F32))
        slots = [psum[:, 1024 * i:1024 * (i + 1)] for i in range(3)]
        o_bank = ctx.enter_context(nc.psum_tensor("o_bank", [P, S], F32))
        aux = ctx.enter_context(nc.psum_tensor("aux_bank", [P, S], F32))

        loaded = {pack: sem("loaded_" + pack) for pack in PACKS}
        up_loaded, x_first, x_rest = sem("up_loaded"), sem("x_first"), sem("x_rest")
        tables_loaded = sem("tables_loaded")
        pool_consts, dve_consts, mu_ready = sem("pool_consts"), sem("dve_consts"), sem("mu_ready")
        w_summed = sem("w_summed")
        scores_done = sem("scores_done")
        diag_done = sem("diag_done")
        exp_done = sem("exp_done")
        products_done = sem("products_done")
        aux_filled = sem("aux_filled")
        aux_emptied = sem("aux_emptied")
        o_copied = sem("o_copied")
        roped = {QM: sem("roped_q"), KP: sem("roped_k")}
        part_step = [sem(f"part_step_{v}") for v in range(4)]
        parts_done = [sem(f"parts_done_{v}") for v in range(4)]
        stacked = [[sem(f"stacked_{v}_{half}") for half in range(2)] for v in range(4)]
        squared = sem("squared")
        stacks_zeroed = [sem("stacks_zeroed_0"), sem("stacks_zeroed_1")]
        v_placed = [sem("v_placed_0"), sem("v_placed_1")]
        ln_steps = ("stats", "parts", "squares", "var_sum", "var", "rstd", "normed")
        lns = {side: {n: sem(f"{side}_{n}_done") for n in ln_steps}
               for side in ("pre", "post")}
        inv_done = sem("inv_done")
        prev_scaled_k, prev_scaled_r = sem("prev_scaled_k"), sem("prev_scaled_r")
        mixed_k, mixed_r = sem("mixed_k"), sem("mixed_r")
        k_acted = sem("k_acted")
        x_done = sem("x_done")
        stored = sem("stored")
        passed = {engine: sem("passed_" + engine) for engine in ("sync", "vector")}
        norms_moved, bound_step, flag_done = sem("norms_moved"), sem("bound_step"), sem("flag_done")
        general_sems = {n: sem("g_" + n) for n in GENERAL_SEMS}
        block = ctx.enter_context(nc.Block())

        def xb(b):
            return X[:, b, :, :].rearrange("p t d -> p (t d)")

        def tail_copied(name):
            return aux_before(2 * B) + AUX_TAIL.index(name) + 1

        def copied(job, name):
            return aux_index(job, name) + 1

        def loops(eng, body):
            body(Job("A", None, 1, 0))
            with eng.Fori(0, 2) as it:
                for r in range(3):
                    body(Job("A", it, 3, 1 + r))
            body(Job("A", None, 1, B - 1))
            body(Job("B", None, 1, 0))
            with eng.Fori(0, B - 2) as it:
                body(Job("B", it, 1, 1))
            body(Job("B", None, 1, B - 1))

        def general(eng, program):
            eng.wait_ge(flag_done, 1)
            needed = eng.value_load(flag[0:1, 0:1], min_val=0, max_val=1)
            with eng.If(needed):
                program(eng)

        def zero_stack(eng, v, half):
            eng.memset(stacks[v][:, half, :, :].rearrange("p h q -> p (h q)").bitcast(F32), 0.0)\
               .then_inc(stacks_zeroed[half], 1)

        def slot_groups(kind, u):
            if kind == "A" or u % 2 == 0:
                return (0, 1, 2), (3,)
            return (0, 1), ()

        def chunk_in_job(kind, u, c):
            return 4 * u + c if kind == "A" else 6 * (u // 2) + 4 * (u % 2) + c

        s = general_sems
        ATT = {0: 0, 2: 1}
        FFN = {1: 0, 3: 1}
        ident = w["identity"]
        g = {"decay": probs[:, 0, :, 0:S], "causal": probs[:, 0, :, S:2 * S]}
        stats, normed, xt = ln["pre"]["stats"], ln["pre"]["normed"], ln["post"]["xt"]
        mean_sum, mean_dif, m2_sum, mean, dif_sq, var_p, var_eps, rstd = [ln["pre"][n] for n in ln_names]
        q_t, k_t, rot, q_head = folded
        w1, w2 = rest
        v_sb = v_stage
        g_probs, relu_g = part_r, relu_k
        probs_t = probs[:, 1, 0, 0:S].rearrange("p (t d) -> p t d", d=P)
        row_max, neg_max, row_sum, row_inv = [inv_sum[:, i, 0:1] for i in range(4)]
        o_sb = o_tok
        ps_t, ps_q, ps_k, ps_v, ps_q2, ps_k2 = [psum[:, S * i:S * (i + 1)] for i in range(6)]
        ps_s, ps_o = o_bank[:], aux

        def head_mask(h):
            at = sum(cols for name, cols in PACK_REST[:[m[0] for m in PACK_REST].index("head_mask")])
            return packs["rest"][:, bass.ds(h + at, 1)]

        def general_sync(sp):
            sp.dma_start(g["decay"], dram["decay"]).then_inc(s["tables_loaded"], 16)
            sp.dma_start(g["causal"], dram["causal"]).then_inc(s["tables_loaded"], 16)
            sp.dma_start(X[:], dram["x"].rearrange("b (t p) d -> p b t d", p=P)).then_inc(s["x_loaded"], 16)
            sp.wait_ge(s["x_done"], 4 * B)
            sp.dma_start(out.rearrange("b (t p) d -> p b t d", p=P), X[:]).then_inc(s["stored"], 16)
            sp.wait_ge(s["stored"], 16)

        def general_pool(pool):
            for phase in range(4):
                with pool.Fori(0, B) as b:
                    n = b + (phase * B + 1)
                    pool.wait_ge(s["var_done"], n)
                    pool.tensor_tensor(rstd[:], var_eps[:], minus_half[:], ALU.pow).then_inc(s["rstd_done"], 1)

        def general_act(act):
            for phase in range(4):
                with act.Fori(0, B) as b:
                    if phase in ATT:
                        with act.Fori(0, H) as h:
                            for qt in range(TILES):
                                m = ((ATT[phase] * B + b) * H + h) * TILES + (qt + 1)
                                act.wait_ge(s["max_done"], m)
                                act.activation(g_probs[:], w2[:], ACT.Exp, bias=neg_max).then_inc(s["exp_done"], 1)
                    else:
                        act.wait_ge(s["ffn_done"], b + (FFN[phase] * B + 1))
                        act.activation(gate[:], ps_q, ACT.Tanh, scale=0.5).then_inc(s["gate_done"], 1)

        def general_pe(pe):
            def transposed(n):
                pe.wait_ge(s["normed_done"], n)
                for t in range(TILES):
                    last = pe.transpose(ps_t[:, t * P:(t + 1) * P], normed[:, t, :], ident)
                last.then_inc(s["xt_done"], 1)

            for phase in range(4):
                with pe.Fori(0, B) as b:
                    n = b + (phase * B + 1)
                    transposed(n)
                    if phase in ATT:
                        a = ATT[phase]
                        na = b + (a * B + 1)
                        pe.wait_ge(s["xt_copied"], n)
                        xs = xt[:, 1:1 + S]
                        wq, wk = (w["wq_a"], w_kk[:]) if a == 0 else (w["wq_b"], w["wk_b"])
                        wv, nv = (w_vv[:], P) if a == 0 else (w["wv_b"], HD)
                        pe.matmul(ps_q, wq, xs, start=True, stop=True)
                        pe.matmul(ps_k, wk, xs, start=True, stop=True)
                        if a:
                            pe.matmul(ps_q2, w["wq_b_swapped"], xs, start=True, stop=True)
                            pe.matmul(ps_k2, w["wk_b_swapped"], xs, start=True, stop=True)
                        for t in range(TILES):
                            last = pe.matmul(ps_v[:, t * P:t * P + nv], xt[:, 1 + t * P:1 + (t + 1) * P], wv,
                                             start=True, stop=True)
                        last.then_inc(s["proj_done"], 1)
                        with pe.Fori(0, H) as h:
                            pe.wait_ge(s["proj_copied"], na)
                            pe.wait_ge(s["head_picked"], (a * B + b) * H + h + 1)
                            for qt in range(TILES):
                                m = ((a * B + b) * H + h) * TILES + (qt + 1)
                                pe.matmul(ps_s, q_head[:, qt * P:(qt + 1) * P], k_t[:], start=True, stop=True)\
                                  .then_inc(s["scores_done"], 1)
                                pe.wait_ge(s["exp_done"], m)
                                for t in range(TILES):
                                    last = pe.transpose(ps_t[:, t * P:(t + 1) * P], g_probs[:, t * P:(t + 1) * P], ident)
                                last.then_inc(s["pt_done"], 1)
                                pe.wait_ge(s["pt_copied"], m)
                                for t in range(TILES):
                                    v = v_sb[:, t, bass.ds(h * HD, HD)] if a == 0 else v_sb[:, t, 0:HD]
                                    last = pe.matmul(ps_o[:, 0:HD], probs_t[:, t, :], v,
                                                     start=(t == 0), stop=(t == TILES - 1))
                                last.then_inc(s["o_done"], 1)
                                pe.wait_ge(s["o_scaled"], m)
                        for t in range(TILES):
                            last = pe.transpose(ps_t[:, t * P:(t + 1) * P], o_sb[:, t, :], ident)
                        last.then_inc(s["ot_done"], 1)
                        pe.wait_ge(s["ot_copied"], na)
                        wo = w["wo_a"] if a == 0 else w["wo_b"]
                        for t in range(TILES):
                            last = pe.matmul(ps_v[:, t * P:(t + 1) * P], o_t[:, t * P:(t + 1) * P], wo,
                                             start=True, stop=True)
                        last.then_inc(s["wo_done"], 1)
                    else:
                        nf = b + (FFN[phase] * B + 1)
                        pe.wait_ge(s["mixed"], nf)
                        pe.matmul(ps_k, w["w_k"], mix_k[:], start=True, stop=True).then_inc(s["k_done"], 1)
                        for t in range(TILES):
                            pe.matmul(ps_q[:, t * P:(t + 1) * P], mix_r[:, t * P:(t + 1) * P], w["w_r"],
                                      start=True, stop=True)
                        pe.wait_ge(s["k_acted"], nf)
                        for t in range(TILES):
                            last = pe.matmul(ps_v[:, t * P:(t + 1) * P], act_k[:, t * P:(t + 1) * P], w["w_v"],
                                             start=True, stop=True)
                        last.then_inc(s["ffn_done"], 1)

        def general_dve(dve):
            dve.wait_ge(s["tables_loaded"], 32)
            dve.wait_ge(s["x_loaded"], 16)
            for phase in range(4):
                with dve.Fori(0, B) as b:
                    n = b + (phase * B + 1)
                    if phase:
                        dve.wait_ge(s["x_done"], n - B)
                    for t in range(TILES):
                        last = dve.bn_stats(stats[:, t, :], X[:, b, t, :])
                    last.then_inc(s["stats_done"], 1)
                    even, odd = stats[:, :, 1], stats[:, :, 4]
                    dve.wait_ge(s["stats_done"], n)
                    dve.tensor_tensor(mean_sum[:], even, odd, ALU.add)
                    dve.tensor_tensor(mean_dif[:], even, odd, ALU.subtract)
                    dve.tensor_tensor(m2_sum[:], stats[:, :, 2], stats[:, :, 5], ALU.add).then_inc(s["parts_done"], 1)
                    dve.wait_ge(s["parts_done"], n)
                    dve.tensor_scalar(mean[:], mean_sum[:], 0.5, None, ALU.mult)
                    dve.tensor_tensor(dif_sq[:], mean_dif[:], mean_dif[:], ALU.mult).then_inc(s["squares_done"], 1)
                    dve.wait_ge(s["squares_done"], n)
                    dve.scalar_tensor_tensor(var_p[:], dif_sq[:], P / 4, m2_sum[:], ALU.mult, ALU.add)\
                       .then_inc(s["var_sum_done"], 1)
                    dve.wait_ge(s["var_sum_done"], n)
                    dve.tensor_scalar(var_eps[:], var_p[:], 1 / P, EPS, ALU.mult, ALU.add).then_inc(s["var_done"], 1)
                    dve.wait_ge(s["rstd_done"], n)
                    for t in range(TILES):
                        last = dve.tensor_scalar(normed[:, t, :], X[:, b, t, :], mean[:, t:t + 1], rstd[:, t:t + 1],
                                                 ALU.subtract, ALU.mult)
                    last.then_inc(s["normed_done"], 1)
                    dve.wait_ge(s["xt_done"], n)
                    dve.tensor_copy(xt[:, 1:1 + S], ps_t).then_inc(s["xt_copied"], 1)
                    if phase in ATT:
                        a = ATT[phase]
                        na = b + (a * B + 1)
                        dve.wait_ge(s["proj_done"], na)
                        if a == 0:
                            dve.tensor_copy(q_t[:], ps_q)
                            dve.tensor_copy(k_t[:], ps_k)
                            dve.tensor_copy(v_sb[:].rearrange("p t d -> p (t d)"), ps_v).then_inc(s["proj_copied"], 1)
                        else:
                            c, sn = w["rope_cos"], w["rope_sin"]
                            k0 = b * 4
                            dve.tensor_tensor(q_t[:], ps_q, c, ALU.mult)
                            dve.tensor_tensor(rot[:], ps_q2, sn, ALU.mult).then_inc(s["rot_step"], 1)
                            dve.wait_ge(s["rot_step"], k0 + 1)
                            dve.tensor_tensor(q_t[:], q_t[:], rot[:], ALU.add).then_inc(s["rot_step"], 1)
                            dve.wait_ge(s["rot_step"], k0 + 2)
                            dve.tensor_tensor(k_t[:], ps_k, c, ALU.mult)
                            dve.tensor_tensor(rot[:], ps_k2, sn, ALU.mult).then_inc(s["rot_step"], 1)
                            dve.wait_ge(s["rot_step"], k0 + 3)
                            dve.tensor_tensor(k_t[:], k_t[:], rot[:], ALU.add).then_inc(s["rot_step"], 1)
                            dve.tensor_copy(v_sb[:, :, 0:HD], ps_v.rearrange("p (t d) -> p t d", d=P)[:, :, 0:HD])\
                               .then_inc(s["proj_copied"], 1)
                        with dve.Fori(0, H) as h:
                            dve.wait_ge(s["proj_copied"], na)
                            mh = (a * B + b) * H + h
                            dve.tensor_scalar(q_head[:], q_t[:], head_mask(h), None, ALU.mult)\
                               .then_inc(s["head_picked"], 1)
                            for qt in range(TILES):
                                m = mh * TILES + (qt + 1)
                                dve.wait_ge(s["scores_done"], m)
                                if a == 0:
                                    dve.tensor_scalar(w1[:], ps_s, SCALE_A, -CLAMP, ALU.mult, ALU.max)\
                                       .then_inc(s["w_step"], 1)
                                    dve.wait_ge(s["w_step"], m)
                                    dve.scalar_tensor_tensor(w2[:], w1[:], CLAMP, g["decay"][:, qt, :], ALU.min, ALU.mult)\
                                       .then_inc(s["weighted"], 1)
                                else:
                                    dve.scalar_tensor_tensor(w2[:], ps_s, SCALE_B, g["causal"][:, qt, :],
                                                             ALU.mult, ALU.min).then_inc(s["weighted"], 1)
                                dve.wait_ge(s["weighted"], m)
                                dve.reduce_max(row_max, w2[:], AX.X).then_inc(s["sum_step"], 1)
                                dve.wait_ge(s["sum_step"], m * 3 - 2)
                                dve.tensor_scalar(neg_max, row_max, -1.0, None, ALU.mult).then_inc(s["max_done"], 1)
                                dve.wait_ge(s["exp_done"], m)
                                dve.reduce_sum(row_sum, g_probs[:], AX.X).then_inc(s["sum_step"], 1)
                                dve.wait_ge(s["sum_step"], m * 3 - 1)
                                dve.reciprocal(row_inv, row_sum).then_inc(s["sum_step"], 1)
                                dve.wait_ge(s["pt_done"], m)
                                dve.tensor_copy(probs[:, 1, 0, 0:S], ps_t).then_inc(s["pt_copied"], 1)
                                dve.wait_ge(s["o_done"], m)
                                dve.wait_ge(s["sum_step"], m * 3)
                                dve.tensor_scalar(o_sb[:, qt, bass.ds(h * HD, HD)], ps_o[:, 0:HD], row_inv, None,
                                                  ALU.mult).then_inc(s["o_scaled"], 1)
                        dve.wait_ge(s["ot_done"], na)
                        dve.tensor_copy(o_t[:], ps_t).then_inc(s["ot_copied"], 1)
                        dve.wait_ge(s["wo_done"], na)
                        dve.tensor_tensor(X[:, b, :, :].rearrange("p t d -> p (t d)"), ps_v,
                                          X[:, b, :, :].rearrange("p t d -> p (t d)"), ALU.add).then_inc(s["x_done"], 1)
                    else:
                        nf = b + (FFN[phase] * B + 1)
                        dve.wait_ge(s["xt_copied"], n)
                        dve.tensor_scalar(part_r[:], xt[:, 0:S], mu_rest[:, 0:1], None, ALU.mult)
                        dve.tensor_scalar(part_k[:], xt[:, 0:S], mu_rest[:, 1:2], None, ALU.mult).then_inc(s["mix_step"], 1)
                        dve.wait_ge(s["mix_step"], nf)
                        dve.scalar_tensor_tensor(mix_r[:], xt[:, 1:1 + S], w["mu_r"], part_r[:], ALU.mult, ALU.add)
                        dve.scalar_tensor_tensor(mix_k[:], xt[:, 1:1 + S], w["mu_k"], part_k[:], ALU.mult, ALU.add)\
                           .then_inc(s["mixed"], 1)
                        dve.wait_ge(s["k_done"], nf)
                        dve.tensor_scalar(relu_k[:], ps_k, 0.0, None, ALU.max).then_inc(s["relu_done"], 1)
                        dve.wait_ge(s["relu_done"], nf)
                        dve.tensor_tensor(act_k[:], relu_k[:], relu_k[:], ALU.mult).then_inc(s["k_acted"], 1)
                        dve.wait_ge(s["gate_done"], nf)
                        dve.scalar_tensor_tensor(gated[:], gate[:], 1.0, ps_v, ALU.add, ALU.mult)\
                           .then_inc(s["gated_done"], 1)
                        dve.wait_ge(s["gated_done"], nf)
                        xb = X[:, b, :, :].rearrange("p t d -> p (t d)")
                        dve.scalar_tensor_tensor(xb, gated[:], 0.5, xb, ALU.mult, ALU.add).then_inc(s["x_done"], 1)

        def store(sp, b, signal):
            sp.dma_start(out[b].rearrange("(t p) d -> p t d", p=P), X[:, b, :, :]).then_inc(signal, 16)

        @block.sync
        def _(sp):
            xs = dram["x"].rearrange("b (t p) d -> p b t d", p=P)
            sp.dma_start(packs["first"][:], dram["pack_first"]).then_inc(loaded["first"], 16)
            sp.dma_start(X[:, 0:1, :, :], xs[:, 0:1]).then_inc(x_first, 16)
            sp.dma_start(w_up[:], dram["w_up"]).then_inc(up_loaded, 16)
            sp.dma_start(packs["fold"][:], dram["pack_fold"]).then_inc(loaded["fold"], 16)
            sp.dma_start(X[:, 1:B, :, :], xs[:, 1:B]).then_inc(x_rest, 16)
            sp.dma_start(norm_sum[:], dram["norm_sum"]).then_inc(tables_loaded, 16)
            sp.dma_start(packs["rest"][:], dram["pack_rest"]).then_inc(loaded["rest"], 16)
            sp.wait_ge(stacks_zeroed[0], 4)

            def stack_half(kind, half, count):
                for v in (QM, KP, QP, KM) if kind == "A" else (KP, QM):
                    for term, part in enumerate(PARTS_OF[v]):
                        if part == 0 and term == 0:
                            sp.wait_ge(part_step[v], count * 3 - 2)
                        if part == 1 and 1 not in PARTS_OF[v][:term]:
                            sp.wait_ge(part_step[v], count * 3)
                        if part == 2:
                            sp.wait_ge(parts_done[v], count)
                        rows = slice(HD * term, HD * term + HD)
                        if kind == "B" and v == KP:
                            dst, src = stacks[v][rows, half, 0, :], parts[v][0:57:8, part, :]
                        else:
                            dst, src = stacks[v][rows, half, :, :], parts[v][64 * half:64 * half + 64, part, :]
                        sp.dma_start(dst, src).then_inc(stacked[v][half], 16)

            def job_dmas(job):
                if job.known:
                    sp.wait_ge(scores_done, job.chunk())
                    sp.sem_inc(passed["sync"], 1)
                else:
                    sp.wait_ge(stacks_zeroed[1], 4)
                stack_half(job.kind, 1, job.n(1))
                if job.known < 2 * B - 1:
                    sp.wait_ge(scores_done, job.chunk(job.chunks // 2))
                    sp.sem_inc(passed["sync"], 1)
                    stack_half(pre_kind(job.known), 0, job.n(2))
                if job.known > B:
                    sp.wait_ge(x_done, job.n())
                    store(sp, job.at(1, -1), stored)

            stack_half("A", 0, 1)
            loops(sp, job_dmas)
            sp.wait_ge(aux_emptied, copied(Job("B", None, 1, B - 1), "norms"))
            sp.dma_start(norm_rows[0:1, 0, :], norms[0:32, :]).then_inc(norms_moved, 16)
            sp.dma_start(norm_rows[0:1, 1, :], norms[32:64, :]).then_inc(norms_moved, 16)
            sp.wait_ge(x_done, 2 * B)
            store(sp, B - 1, stored)
            sp.wait_ge(stored, 16 * B)
            general(sp, general_sync)

        def k_rows(kind):
            return slice(0, P) if kind == "A" else slice(0, 64)

        def split(eng, v, ready, count, rest_buf, before, rows=slice(0, P)):
            src, dst, rest_of = folded[v][rows, :], parts[v][rows, :, :], rest_buf[rows, :]

            def rounded(to, of):
                if eng is nc.gpsimd:
                    ones = bass.AP(one, 0, [[1, rows.stop], [0, S]])
                    return eng.tensor_tensor(to, of, ones, ALU.mult)
                return eng.tensor_scalar(to, of, 1.0, None, ALU.mult)

            if not isinstance(count, int) or count > 1:
                for half in range(2):
                    eng.wait_ge(stacked[v][half], (count - 1) * (16 * TERMS))
            eng.wait_ge(*ready)
            rounded(dst[:, 0, :], src).then_inc(part_step[v], 1)
            if before is not None:
                eng.wait_ge(parts_done[before[0]], before[1])
            eng.wait_ge(part_step[v], count * 3 - 2)
            eng.tensor_tensor(rest_of, src, dst[:, 0, :], ALU.subtract).then_inc(part_step[v], 1)
            eng.wait_ge(part_step[v], count * 3 - 1)
            rounded(dst[:, 1, :], rest_of).then_inc(part_step[v], 1)
            eng.wait_ge(part_step[v], count * 3)
            eng.tensor_tensor(dst[:, 2, :], rest_of, dst[:, 1, :], ALU.subtract).then_inc(parts_done[v], 1)

        @block.gpsimd
        def _(pool):
            pool.memset(minus_half[:], -0.5).then_inc(pool_consts, 1)
            pool.memset(one[:], 1.0).then_inc(pool_consts, 1)
            for v in (QM, KP):
                zero_stack(pool, v, 0)
            pool.wait_ge(pool_consts, 2)

            def root(side, count):
                pool.wait_ge(lns[side]["var"], count)
                pool.tensor_tensor(ln[side]["rstd"][:], ln[side]["var_eps"][:], minus_half[:], ALU.pow)\
                    .then_inc(lns[side]["rstd"], 1)

            def square(kind, k_ready, norms_step):
                pool.wait_ge(*k_ready)
                if norms_step is not None:
                    pool.wait_ge(aux_filled, norms_step + 1)
                q = folded[QP if kind == "A" else QM]
                pool.tensor_tensor(squares[:, 0, :], q[:], q[:], ALU.mult)
                rows = k_rows(kind)
                pool.tensor_tensor(squares[rows, 1, :], folded[KP][rows, :], folded[KP][rows, :], ALU.mult)\
                    .then_inc(squared, 1)

            def act_square(relu_copied):
                pool.wait_ge(aux_emptied, relu_copied)
                pool.tensor_tensor(act_k[:], relu_k[:], relu_k[:], ALU.mult).then_inc(k_acted, 1)

            def rope_add(v, sin_done):
                other, rows = folded[QP if v == QM else KM], k_rows("B") if v == KP else slice(0, P)
                pool.wait_ge(aux_emptied, sin_done)
                pool.tensor_tensor(folded[v][rows, :], folded[v][rows, :], other[rows, :], ALU.add)\
                    .then_inc(roped[v], 1)

            def add_gated(b, gated_done):
                pool.wait_ge(aux_emptied, gated_done)
                pool.tensor_tensor(xb(b), gated[:], xb(b), ALU.add).then_inc(x_done, 1)

            def pool_job(job):
                nxt, n = pre_kind(job.known), job.known
                roped_count = 1 if n == B - 1 else job.at(1, 2)
                if nxt == "A":
                    q_ready, k_ready = (aux_emptied, copied(job, "q")), (aux_emptied, copied(job, "k"))
                    split(pool, QM, q_ready, job.n(2), rest[0], (QP, job.n(1)))
                    split(pool, QP, q_ready, job.n(2), rest[0], (QM, job.n(2)))
                    if n:
                        root("post", job.n())
                    split(pool, KM, k_ready, job.n(2), rest[1], (KP, job.n(2)))
                    square(nxt, k_ready, aux_index(job, "norms"))
                elif nxt == "B":
                    rope_add(KP, copied(job, "k"))
                    split(pool, KP, (roped[KP], roped_count), job.n(2), rest[1],
                          (KM, B) if n == B - 1 else (KP, job.n(1)), k_rows("B"))
                    root("post", job.n())
                    rope_add(QM, copied(job, "q_swapped"))
                    split(pool, QM, (roped[QM], roped_count), job.n(2), rest[0],
                          (QP, B) if n == B - 1 else (QM, job.n(1)))
                else:
                    root("post", job.n())
                if n:
                    act_square(copied(job, "ffn_k"))
                if nxt == "A":
                    root("pre", job.n(3))
                if n and nxt != "B":
                    add_gated(job.at(1, -1) if n != B else B - 1, copied(job, "ffn_v"))
                if nxt == "B":
                    square(nxt, (roped[KP], roped_count), aux_index(job, "norms"))
                    root("pre", job.n(3))
                    add_gated(job.at(1, -1) if n != B else B - 1, copied(job, "ffn_v"))

            root("pre", 1)
            for v in (QP, KM):
                zero_stack(pool, v, 0)
            q_ready = (aux_emptied, AUX_PROLOGUE.index("q") + 1)
            split(pool, QM, q_ready, 1, rest[0], None)
            split(pool, QP, q_ready, 1, rest[0], (QM, 1))
            k_ready = (aux_emptied, AUX_PROLOGUE.index("k") + 1)
            split(pool, KM, k_ready, 1, rest[1], (KP, 1))
            square("A", k_ready, None)
            root("pre", 2)
            loops(pool, pool_job)
            root("post", 2 * B)
            act_square(tail_copied("ffn_k"))
            add_gated(B - 1, tail_copied("ffn_v"))
            general(pool, general_pool)

        @block.scalar
        def _(act):
            def copy_o(half, bursts):
                act.wait_ge(products_done, bursts)
                act.activation(o_raw[:, half, :], o_bank[:], ACT.Copy).then_inc(o_copied, 1)

            def step(name, index):
                dst = {"pre_xt": ln["pre"]["xt"][:, 1:1 + S], "post_xt": ln["post"]["xt"][:, 1:1 + S],
                       "o_t": o_t[:], "ffn_r": gate[:]}.get(name)
                if dst is not None:
                    act.wait_ge(aux_filled, index + 1)
                    fn, scale = (ACT.Tanh, 0.5) if name == "ffn_r" else (ACT.Copy, 1.0)
                    act.activation(dst, aux[:], fn, scale=scale).then_inc(aux_emptied, 1)

            def act_job(job):
                scale = SCALE_A if job.kind == "A" else SCALE_B
                steps = aux_steps(job.known)

                def exps(u, chunks):
                    for c in chunks:
                        k = chunk_in_job(job.kind, u, c)
                        slot = slots[job.slot_of(k)]
                        act.wait_ge(diag_done, job.chunk(k + 1))
                        if job.kind == "A":
                            dst, src = probs[:, u % 2, c, :], slot
                        elif u % 2 == 0:
                            dst, src = probs[:, 0, c, 0:896], slot[:, 0:896]
                        else:
                            dst = probs[:, 1, 2 * c:2 * c + 2, 0:384]
                            src = slot.rearrange("p (h q) -> p h q", h=2)[:, :, 0:384]
                        act.activation(dst, src, ACT.Exp, scale=scale).then_inc(exp_done, 1)

                def steps_at(u, where):
                    for su, place, name in steps:
                        if (su, place) == (u, where):
                            step(name, aux_index(job, name))

                for u in range(8):
                    first, second = slot_groups(job.kind, u)
                    steps_at(u, "a")
                    ahead = 1 if job.kind == "B" else 2
                    exps(u, first[:ahead])
                    steps_at(u, "b")
                    exps(u, first[ahead:])
                    if u == 0 and job.known:
                        copy_o(1, job.burst())
                    if u == 4:
                        copy_o(0, job.burst(4))
                    exps(u, second)

            step("pre_xt", AUX_PROLOGUE.index("pre_xt"))
            loops(act, act_job)
            copy_o(1, 16 * B)
            for k, name in enumerate(AUX_TAIL):
                step(name, aux_before(2 * B) + k)
            general(act, general_act)

        @block.tensor
        def _(pe):
            ident = w["identity"]
            def claim(index):
                if not isinstance(index, int) or index > 0:
                    pe.wait_ge(aux_emptied, index)

            def tiles_of(fn):
                for t in range(TILES):
                    last = fn(t, slice(t * P, (t + 1) * P))
                last.then_inc(aux_filled, 1)

            def step(name, kind, index, pre, post, o_count):
                claim(index)
                if name in ("pre_xt", "post_xt"):
                    side, count = ("pre", pre) if name == "pre_xt" else ("post", post)
                    pe.wait_ge(lns[side]["normed"], count)
                    tiles_of(lambda t, c: pe.transpose(aux[:, c], ln[side]["normed"][:, t, :], ident))
                elif name in ("q", "k", "q_swapped"):
                    weight = {"qA": w["wq_a"], "kA": w_kk[:], "qB": w["wq_b"], "kB": w["wk_b_pair"],
                              "q_swappedB": w["wq_b_swapped"]}[name + kind]
                    pe.matmul(aux[:], weight, ln["pre"]["xt"][:, 1:1 + S], start=True, stop=True).then_inc(aux_filled, 1)
                elif name == "v":
                    wv, nv = (w_vv[:], P) if kind == "A" else (w["wv_b"], HD)
                    tiles_of(lambda t, c: pe.matmul(aux[:, t * P:t * P + nv], ln["pre"]["xt"][:, 1 + t * P:1 + (t + 1) * P],
                                                    wv, start=True, stop=True))
                elif name == "norms":
                    pe.wait_ge(squared, o_count)
                    rows, of_k = (slice(0, P), 0) if kind == "A" else (slice(0, 64), 1)
                    pe.matmul(aux[0:32, :], norm_sum[:, 0, :], squares[:, 0, :], start=True, stop=True)
                    pe.matmul(aux[32:64, :], norm_sum[rows, of_k, :], squares[rows, 1, :], start=True, stop=True)\
                      .then_inc(aux_filled, 1)
                elif name in ("o_first", "o_second"):
                    half = int(name == "o_second")
                    pe.wait_ge(o_copied, o_count)
                    tiles_of(lambda t, c: pe.transpose(aux[:, c], o_raw[:, half, c], ident))
                elif name == "o_t":
                    tiles_of(lambda t, c: pe.transpose(aux[:, c], o_tok[:, t, :], ident))
                elif name == "wo":
                    tiles_of(lambda t, c: pe.matmul(aux[:, c], o_t[:, c], w["wo_a" if kind == "A" else "wo_b"],
                                                    start=True, stop=True))
                elif name == "ffn_k":
                    pe.wait_ge(mixed_k, post)
                    pe.matmul(aux[:], w["w_k"], mix_k[:], start=True, stop=True).then_inc(aux_filled, 1)
                elif name == "ffn_r":
                    pe.wait_ge(mixed_r, post)
                    tiles_of(lambda t, c: pe.matmul(aux[:, c], mix_r[:, c], w["w_r"], start=True, stop=True))
                elif name == "ffn_v":
                    pe.wait_ge(k_acted, post)
                    tiles_of(lambda t, c: pe.matmul(aux[:, c], act_k[:, c], w_v_half[:], start=True, stop=True))

            def scores(job, u, c):
                half, second = u // 4, u // 2 % 2
                k = chunk_in_job(job.kind, u, c)
                slot = slots[job.slot_of(k)]
                if k or job.known:
                    if job.known or k >= 3:
                        pe.wait_ge(exp_done, job.chunk(k - 2))
                if c == 0 and u % 4 == 0:
                    for v in (QM, KP, QP, KM) if job.kind == "A" else (QM, KP):
                        pe.wait_ge(stacked[v][half], job.n(1) * (16 * TERMS))
                if job.kind == "A":
                    head = 2 * c + second
                    for i in range(2):
                        kt = 2 * (u % 2) + i
                        keys, edge = slice(kt * P, (kt + 1) * P), kt * P
                        bank = slot[:, i * S:(i + 1) * S]
                        if kt:
                            last = pe.matmul(bank[:, 0:edge], stacks[KM][:, half, head, keys],
                                             stacks[QP][:, half, head, 0:edge], start=True, stop=True)
                        last = pe.matmul(bank[:, edge:S], stacks[KP][:, half, head, keys],
                                         stacks[QM][:, half, head, edge:S], start=True, stop=True)
                else:
                    if u % 2 == 0:
                        rows = [(0, 2 * c + second, 0), (1, 2 * c + second, S)]
                    else:
                        rows = [(kt, 2 * (2 * c + i) + second, i * S + (kt - 2) * 2 * P)
                                for i in range(2) for kt in (2, 3)]
                    for kt, head, col in rows:
                        last = pe.matmul(slot[:, col:col + S - kt * P], stacks[KP][:, half, 0, kt * P:(kt + 1) * P],
                                         stacks[QM][:, half, head, kt * P:S], start=True, stop=True)
                last.then_inc(scores_done, 1)

            def products(kind, u, exp_count, job_count):
                half, second, pair = u // 4, u // 2 % 2, u % 2
                pe.wait_ge(exp_done, exp_count)
                if u % 4 == 0:
                    pe.wait_ge(v_placed[half], job_count)
                    if half or not isinstance(job_count, int) or job_count > 1:
                        pe.wait_ge(o_copied, job_count * 2 - 2 + half)
                for i in range(2):
                    kt = 2 * pair + i
                    q0, col = (0, i * S) if kind == "A" else (kt * P, i * (2 * P if pair else S))
                    for g in range(GROUPS):
                        last = pe.matmul(o_bank[32 * g:32 * g + 32, q0:S], v_heads[:, half, kt, 2 * g + second, :],
                                         probs[:, u % 2, g, col:col + S - q0],
                                         start=(u % 4 == 0 and i == 0), stop=(u % 4 == 3 and i == 1))
                last.then_inc(products_done, 1)

            def pe_job(job):
                steps = aux_steps(job.known)

                def aux_at(u, place):
                    for su, sp_, name in steps:
                        if (su, sp_) == (u, place):
                            kind = job.kind if name == "norms" else \
                                pre_kind(job.known) if name in ("q", "k", "v", "q_swapped") else \
                                "A" if job.known <= B else "B"
                            o_count = {"norms": job.n(1), "o_first": job.at(2, (0 if job.kind == "A" else 2 * B) + 1),
                                       "o_second": job.at(2, 0 if job.kind == "A" else 2 * B)}.get(name)
                            step(name, kind, aux_index(job, name), job.n(2), job.n(), o_count)

                for u in range(8):
                    first, second = slot_groups(job.kind, u)
                    aux_at(u, "a")
                    for c in first:
                        scores(job, u, c)
                    aux_at(u, "b")
                    if u:
                        products(job.kind, u - 1, job.chunk(chunk_in_job(job.kind, u, 0)), job.n(1))
                    elif job.known:
                        products("A" if job.known <= B else "B", 7, job.chunk(), job.n())
                    for c in second:
                        scores(job, u, c)

            def keep_warm(count):
                for _ in range(count):
                    pe.matmul(slots[2][:, 0:P], ident, ident, start=True, stop=True)

            pe.wait_ge(loaded["first"], 16)
            pe.wait_ge(w_summed, 1)
            pe.transpose(aux[:, 0:P], w_sum[:], ident).then_inc(aux_filled, 1)
            claim(1)
            pe.matmul(aux[0:LAT, 0:P], w["w_down"], w_sum_t[:], start=True, stop=True).then_inc(aux_filled, 1)
            for k, name in enumerate(AUX_PROLOGUE):
                if k > 2:
                    keep_warm(4)
                if name in ("pre_xt", "q", "k", "v"):
                    step(name, "A", k, 1, None, None)
                elif name in ("w_kk", "w_vv"):
                    claim(k)
                    pe.wait_ge(up_loaded, 16)
                    pe.matmul(aux[:, 0:P], w_lat_t[:], w_up[:, UP_K if name == "w_kk" else UP_V, :],
                              start=True, stop=True).then_inc(aux_filled, 1)
            pe.wait_ge(tables_loaded, 16)
            pe.wait_ge(loaded["rest"], 16)
            pe.wait_ge(mu_ready, 3)
            pe.wait_ge(stacked[KP][0], 16 * TERMS)
            keep_warm(16)
            loops(pe, pe_job)
            products("B", 7, 56 * B, 2 * B)
            for k, name in enumerate(AUX_TAIL):
                keep_warm((2, 2, 3, 20, 4, 4, 0)[k])
                step(name, "B", aux_before(2 * B) + k, None, 2 * B, 4 * B)
            general(pe, general_pe)

        def flat_ap(tensor, offset, *dims):
            width = int(np.prod(tensor.shape[1:]))
            return bass.AP(tensor, offset, [[width, P], *[list(d) for d in dims]])

        def table_ap(name, *repeats):
            at = 0
            for member, cols in PACK_REST:
                if member == name:
                    break
                at += cols
            return flat_ap(packs["rest"], at, *[(0, r) for r in repeats], (1, P))

        @block.vector
        def _(dve):
            def filled(index):
                dve.wait_ge(aux_filled, index + 1)

            def diagonal(job, u, c):
                k = chunk_in_job(job.kind, u, c)
                at = 1024 * job.slot_of(k)
                if job.kind == "A":
                    blocks = flat_ap(psum, at + 256 * (u % 2), (S + P, 2), (1, P))
                    table, op = table_ap("diag_decay", 2), ALU.mult
                elif u % 2 == 0:
                    blocks = flat_ap(psum, at, (S, 2), (1, P))
                    table, op = table_ap("diag_causal", 2), ALU.min
                else:
                    blocks = flat_ap(psum, at, (S, 2), (2 * P, 2), (1, P))
                    table, op = table_ap("diag_causal", 2, 2), ALU.min
                dve.wait_ge(scores_done, job.chunk(k + 1))
                dve.tensor_tensor(blocks, blocks, table, op).then_inc(diag_done, 1)

            def ln_stats(side, b, count):
                t_, s_ = ln[side], lns[side]
                for t in range(TILES):
                    last = dve.bn_stats(t_["stats"][:, t, :], X[:, b, t, :])
                last.then_inc(s_["stats"], 1)
                even, odd = t_["stats"][:, :, 1], t_["stats"][:, :, 4]
                dve.wait_ge(s_["stats"], count)
                dve.tensor_tensor(t_["mean_sum"][:], even, odd, ALU.add)
                dve.tensor_tensor(t_["mean_dif"][:], even, odd, ALU.subtract)
                dve.tensor_tensor(t_["m2_sum"][:], t_["stats"][:, :, 2], t_["stats"][:, :, 5], ALU.add)\
                   .then_inc(s_["parts"], 1)
                dve.wait_ge(s_["parts"], count)
                dve.tensor_scalar(t_["mean"][:], t_["mean_sum"][:], 0.5, None, ALU.mult)
                dve.tensor_tensor(t_["dif_sq"][:], t_["mean_dif"][:], t_["mean_dif"][:], ALU.mult)\
                   .then_inc(s_["squares"], 1)
                dve.wait_ge(s_["squares"], count)
                dve.scalar_tensor_tensor(t_["var_p"][:], t_["dif_sq"][:], P / 4, t_["m2_sum"][:], ALU.mult, ALU.add)\
                   .then_inc(s_["var_sum"], 1)
                dve.wait_ge(s_["var_sum"], count)
                dve.tensor_scalar(t_["var_eps"][:], t_["var_p"][:], 1 / P, EPS, ALU.mult, ALU.add)\
                   .then_inc(s_["var"], 1)

            def ln_normalise(side, b, count):
                t_, s_ = ln[side], lns[side]
                dve.wait_ge(s_["rstd"], count)
                for t in range(TILES):
                    last = dve.tensor_scalar(t_["normed"][:, t, :], X[:, b, t, :], t_["mean"][:, t:t + 1],
                                             t_["rstd"][:, t:t + 1], ALU.subtract, ALU.mult)
                last.then_inc(s_["normed"], 1)

            def folded_free(variants, count):
                if not isinstance(count, int) or count > 1:
                    for v in variants:
                        dve.wait_ge(parts_done[v], count - 1)
                    dve.wait_ge(squared, count - 1)

            def fold(variants, index, count):
                folded_free(variants, count)
                filled(index)
                for v in variants:
                    table = w["fold_down" if v in (QM, KM) else "fold_up"]
                    last = dve.tensor_tensor(folded[v][:], aux[:], table, ALU.mult)
                last.then_inc(aux_emptied, 1)

            def rope_cos(index, count):
                folded_free([QM], count)
                filled(index)
                dve.tensor_tensor(folded[QM][:], aux[:], w["rope_cos"], ALU.mult).then_inc(aux_emptied, 1)

            def rope_sin(index, first):
                if first:
                    dve.wait_ge(parts_done[QP], B)
                filled(index)
                dve.tensor_tensor(folded[QP][:], aux[:], w["rope_sin"], ALU.mult).then_inc(aux_emptied, 1)

            def rope_k(index, count, first):
                folded_free([KP], count)
                if first:
                    dve.wait_ge(parts_done[KM], B)
                filled(index)
                dve.tensor_tensor(folded[KP][0:64, :], aux[0:64, :], w["rope_cos"][0:64, :], ALU.mult)
                dve.tensor_tensor(folded[KM][0:64, :], aux[64:P, :], w["rope_sin"][64:P, :], ALU.mult)\
                   .then_inc(aux_emptied, 1)

            def stage_v(kind, index, count):
                if not isinstance(count, int) or count > 1:
                    for half in range(2):
                        dve.wait_ge(v_placed[half], count - 1)
                filled(index)
                nv = P if kind == "A" else HD
                dve.tensor_copy(v_stage[:, :, 0:nv], aux[:].rearrange("p (t d) -> p t d", d=P)[:, :, 0:nv])\
                   .then_inc(aux_emptied, 1)

            def place_v(kind, half, staged, bursts):
                if not isinstance(bursts, int) or bursts > 0:
                    dve.wait_ge(products_done, bursts)
                dve.wait_ge(aux_emptied, staged)
                for second in range(2):
                    if kind == "A":
                        src = flat_ap(v_stage, 64 * half + HD * second, (P, TILES), (2 * HD, GROUPS), (1, HD))
                    else:
                        src = flat_ap(v_stage, 0, (P, TILES), (0, GROUPS), (1, HD))
                    dst = v_heads[:, half, :, second::2, HD * second:HD * second + HD]
                    last = dve.tensor_copy(dst, src)
                last.then_inc(v_placed[half], 1)

            def normalise_o(half, index, count):
                cols = aux[:].rearrange("p (g c) -> p g c", c=32)
                filled(index)
                dve.reciprocal(inv_sum[:], cols[:, :, 2 * HD:2 * HD + 2]).then_inc(inv_done, 1)
                dve.wait_ge(inv_done, count)
                for second in range(2):
                    dst = flat_ap(o_tok, 64 * half + HD * second, (P, TILES), (2 * HD, GROUPS), (1, HD))
                    src = flat_ap(aux, HD * second, (P, TILES), (32, GROUPS), (1, HD))
                    inv = flat_ap(inv_sum, second, (2 * GROUPS, TILES), (2, GROUPS), (0, HD))
                    last = dve.tensor_tensor(dst, src, inv, ALU.mult)
                last.then_inc(aux_emptied, 1)

            def add_attention(b, index):
                filled(index)
                dve.tensor_tensor(xb(b), aux[:], xb(b), ALU.add).then_inc(aux_emptied, 1)
                dve.wait_ge(aux_emptied, index + 1)
                dve.sem_inc(passed["vector"], 1)

            def mix(which, xt_copied, count):
                dst, part, mu, scaled, signal = ((mix_k, part_k, "mu_k", prev_scaled_k, mixed_k),
                                                 (mix_r, part_r, "mu_r", prev_scaled_r, mixed_r))[which]
                rest_of = mu_rest[:, 1 - which:2 - which]
                dve.wait_ge(aux_emptied, xt_copied)
                dve.tensor_scalar(part[:], ln["post"]["xt"][:, 0:S], rest_of, None, ALU.mult).then_inc(scaled, 1)
                dve.wait_ge(scaled, count)
                dve.scalar_tensor_tensor(dst[:], ln["post"]["xt"][:, 1:1 + S], w[mu], part[:], ALU.mult, ALU.add)\
                   .then_inc(signal, 1)

            def relu(index):
                filled(index)
                dve.tensor_scalar(relu_k[:], aux[:], 0.0, None, ALU.max).then_inc(aux_emptied, 1)

            def gate_ffn(index):
                filled(index)
                dve.scalar_tensor_tensor(gated[:], gate[:], 1.0, aux[:], ALU.add, ALU.mult).then_inc(aux_emptied, 1)

            def side_work(job, u, place):
                n, nxt, idx = job.known, pre_kind(job.known), lambda name: aux_index(job, name)
                prev_b = job.at(1, -1) if n != B else B - 1
                later_b = (n + 2) % B if job.it is None else job.at(1, 2) % B
                at = (u, place)
                if at == (0, "early"):
                    filled(idx("norms"))
                    dve.reduce_max(norms[:, bass.ds(job.n(), 1)], aux[0:64, :], AX.X).then_inc(aux_emptied, 1)
                if at == (1, "late"):
                    if nxt == "A":
                        fold((KP, KM), idx("k"), job.n(2))
                    if nxt == "B":
                        rope_k(idx("k"), job.n(2), n == B - 1)
                    staged = AUX_PROLOGUE.index("v") + 1 if n == 0 else copied_before(job, "v")
                    place_v(job.kind, 1, staged, job.burst())
                if at == (2, "early") and n:
                    normalise_o(1, idx("o_second"), job.n() * 2)
                if at == (6, "late") and nxt:
                    place_v(nxt, 0, copied(job, "v"), job.burst(4))
                if at == ((6, "mid") if nxt == "A" else (6, "late")) and nxt:
                    if n > 1:
                        dve.wait_ge(x_done, job.n(-1))
                    ln_stats("pre", later_b, job.n(3))
                if nxt == "A":
                    if at == (1, "early"):
                        fold((QM, QP), idx("q"), job.n(2))
                    if at == (2, "late"):
                        split(dve, KP, (aux_emptied, copied(job, "k")), job.n(2), rest[1], (KM, job.n(1)))
                    if at == (3, "early") and n:
                        add_attention(prev_b, idx("wo"))
                    if at == (3, "late") and n:
                        ln_stats("post", prev_b, job.n())
                    if at == (4, "mid") and n:
                        ln_normalise("post", prev_b, job.n())
                    if at == (4, "late"):
                        stage_v("A", idx("v"), job.n(2))
                    if at == (5, "late"):
                        if n:
                            mix(0, copied(job, "post_xt"), job.n())
                        normalise_o(0, idx("o_first"), job.n() * 2 + 1)
                        if n:
                            mix(1, copied(job, "post_xt"), job.n())
                    if at == (6, "early") and n:
                        relu(idx("ffn_k"))
                    if at == (7, "early") and n:
                        gate_ffn(idx("ffn_v"))
                    if at == (7, "late"):
                        ln_normalise("pre", later_b, job.n(3))
                    return
                if nxt and at == (1, "early"):
                    rope_cos(idx("q"), job.n(2))
                if nxt and at == (3, "early"):
                    rope_sin(idx("q_swapped"), n == B - 1)
                if at == (3, "late"):
                    add_attention(prev_b, idx("wo"))
                    ln_stats("post", prev_b, job.n())
                if at == (4, "late"):
                    if nxt:
                        stage_v("B", idx("v"), job.n(2))
                    ln_normalise("post", prev_b, job.n())
                if at == (5, "late"):
                    mix(0, copied(job, "post_xt"), job.n())
                    mix(1, copied(job, "post_xt"), job.n())
                if at == (6, "early"):
                    relu(idx("ffn_k"))
                if at == (7, "late"):
                    normalise_o(0, idx("o_first"), job.n() * 2 + 1)
                    if nxt:
                        ln_normalise("pre", later_b, job.n(3))
                if at == (7, "early"):
                    gate_ffn(idx("ffn_v"))

            def copied_before(job, name):
                n = job.known - 1
                k = [s[2] for s in aux_steps(n)].index(name)
                back = len(aux_steps(n)) - k
                return aux_before(job.known) - back + 1 if job.it is None else job.aux(1 - back)

            def dve_job(job):
                for u in range(8):
                    first, second = slot_groups(job.kind, u)
                    side_work(job, u, "early")
                    for c in first[:-1]:
                        diagonal(job, u, c)
                    side_work(job, u, "mid")
                    diagonal(job, u, first[-1])
                    side_work(job, u, "late")
                    for c in second:
                        diagonal(job, u, c)

            dve.memset(ln["post"]["xt"][:, 0:1], 0.0).then_inc(dve_consts, 1)
            dve.memset(v_heads[:], 0.0).then_inc(dve_consts, 1)
            dve.wait_ge(dve_consts, 2)
            for second in range(2):
                dve.memset(v_heads[:, :, :, second::2, 2 * HD + second:2 * HD + second + 1], 1.0).then_inc(dve_consts, 1)
            dve.wait_ge(loaded["first"], 16)
            dve.tensor_tensor(w_sum[:], w["wk_a"], w["wv_a"], ALU.add).then_inc(w_summed, 1)
            dve.wait_ge(x_first, 16)
            ln_stats("pre", 0, 1)
            def copy_out(name, dst, src):
                filled(AUX_PROLOGUE.index(name))
                dve.tensor_copy(dst, src).then_inc(aux_emptied, 1)

            copy_out("w_sum_t", w_sum_t[:], aux[:, 0:P])
            copy_out("w_lat_t", w_lat_t[:], aux[0:LAT, 0:P])
            ln_normalise("pre", 0, 1)
            dve.wait_ge(loaded["fold"], 16)
            fold((QM, QP), AUX_PROLOGUE.index("q"), 1)
            copy_out("w_kk", w_kk[:], aux[:, 0:P])
            copy_out("w_vv", w_vv[:], aux[:, 0:P])
            fold((KP, KM), AUX_PROLOGUE.index("k"), 1)
            k_ready = (aux_emptied, AUX_PROLOGUE.index("k") + 1)
            split(dve, KP, k_ready, 1, rest[1], None)
            dve.wait_ge(dve_consts, 4)
            stage_v("A", AUX_PROLOGUE.index("v"), 1)
            place_v("A", 0, AUX_PROLOGUE.index("v") + 1, 0)
            dve.wait_ge(loaded["rest"], 16)
            for i, mu in enumerate(("mu_r", "mu_k")):
                dve.tensor_scalar(mu_rest[:, i:i + 1], w[mu], -1.0, 1.0, ALU.mult, ALU.add).then_inc(mu_ready, 1)
            dve.tensor_scalar(w_v_half[:], w["w_v"], 0.5, None, ALU.mult).then_inc(mu_ready, 1)
            dve.wait_ge(x_rest, 16)
            ln_stats("pre", 1, 2)
            dve.wait_ge(mu_ready, 3)
            for v in range(4):
                zero_stack(dve, v, 1)
            ln_normalise("pre", 1, 2)
            loops(dve, dve_job)
            b = B - 1
            at = {name: aux_before(2 * B) + k for k, name in enumerate(AUX_TAIL)}
            normalise_o(1, at["o_second"], 4 * B)
            add_attention(b, at["wo"])
            ln_stats("post", b, 2 * B)
            ln_normalise("post", b, 2 * B)
            mix(0, at["post_xt"] + 1, 2 * B)
            mix(1, at["post_xt"] + 1, 2 * B)
            relu(at["ffn_k"])
            for kind, scale in ((0, SCALE_A), (1, SCALE_B)):
                dve.memset(norm_rows[0:1, 2, :].rearrange("p (r k b) -> p r k b", k=2, b=B)[:, :, kind, :],
                           float(scale * scale / (LIMIT * LIMIT))).then_inc(bound_step, 1)
            dve.wait_ge(norms_moved, 32)
            for by in (1, 2):
                dve.tensor_tensor(norm_rows[0:1, 0, :], norm_rows[0:1, 0, :], norm_rows[0:1, by, :], ALU.mult)\
                   .then_inc(bound_step, 1)
                dve.wait_ge(bound_step, 2 + by)
            dve.tensor_scalar(norm_rows[0:1, 1, :], norm_rows[0:1, 0, :], 1.0, 0.0, ALU.is_lt, ALU.is_equal)\
               .then_inc(bound_step, 1)
            dve.wait_ge(bound_step, 5)
            dve.reduce_max(flag_f[:], norm_rows[0:1, 1, :], AX.X).then_inc(bound_step, 1)
            dve.wait_ge(bound_step, 6)
            dve.tensor_copy(flag[:], flag_f[:]).then_inc(flag_done, 1)
            gate_ffn(at["ffn_v"])
            general(dve, general_dve)


def tables():
    i = np.arange(S, dtype=np.float32)
    dist = np.abs(i[:, None] - i[None, :])
    decay = np.exp(np.float32(-DECAY) * dist).astype(np.float32)
    causal = np.where(i[:, None] >= i[None, :], np.float32(3.0e38), np.float32(-3.0e38)).astype(np.float32)
    freqs = (np.float32(1.0) / np.float32(1000.0) ** (np.arange(0, HD, 2, dtype=np.float32) / np.float32(HD)))
    ang = i[None, :] * freqs[:, None].astype(np.float32)
    cos, sin = np.cos(ang), np.sin(ang)
    row_d, row_head = row_order()
    k, q = np.arange(P)[:, None].astype(np.float64), np.arange(P)[None, :]
    along = np.arange(S, dtype=np.float64)
    by_tile = lambda m: np.ascontiguousarray(m.reshape(TILES, P, S).transpose(1, 0, 2))
    heads = (row_head[:, None] == np.arange(H)[None, :]).astype(np.float32)
    return {
        "identity": np.eye(P, dtype=np.float32),
        "head_mask": heads,
        "norm_sum": np.stack([np.concatenate([heads, 0 * heads], axis=1),
                              np.concatenate([heads[:, :HALF], heads[:, :HALF], 0 * heads], axis=1)], axis=1),
        "decay": by_tile(decay),
        "causal": by_tile(causal),
        "rope_cos": np.concatenate([cos, cos])[row_d].astype(np.float32),
        "rope_sin": np.concatenate([-sin, sin])[row_d].astype(np.float32),
        "fold_down": np.tile(np.exp(-DECAY * along), (P, 1)).astype(np.float32),
        "fold_up": np.tile(np.exp(DECAY * along), (P, 1)).astype(np.float32),
        "diag_decay": np.exp(-DECAY * (np.abs(q - k) - (q - k))).astype(np.float32),
        "diag_causal": np.where(q >= k, np.float32(3.0e38), np.float32(-3.0e4)).astype(np.float32),
    }


def row_order():
    rows = np.arange(P)
    return rows // HALF % HD, rows // 64 * HALF + rows % HALF


def kernel(**inputs):
    import concourse.bacc as bacc
    from concourse.bass_utils import run_bass_kernel_spmd

    x = {k.removeprefix("L0_"): np.ascontiguousarray(v) for k, v in inputs.items()}
    row_d, row_head = row_order()
    cols = row_head * HD + row_d
    split = np.array([*range(0, HD, 2), *range(1, HD, 2)])
    swap = np.array([*range(1, HD, 2), *range(0, HD, 2)])
    wq_b = x["attn_b_wq"].T
    arrays = {
        "wq_a": x["attn_a_Wq"][:, cols], "wk_a": x["attn_a_Wk"], "wv_a": x["attn_a_Wv"],
        "wo_a": x["attn_a_Wo"], "w_down": x["attn_a_W_down_kv"],
        "wq_b": wq_b[:, row_head * HD + split[row_d]], "wq_b_swapped": wq_b[:, row_head * HD + swap[row_d]],
        "wk_b": x["attn_b_wk"][:, split[row_d]], "wk_b_swapped": x["attn_b_wk"][:, swap[row_d]],
        "wk_b_pair": x["attn_b_wk"][:, np.where(np.arange(P) < 64, split[row_d], swap[row_d])],
        "wv_b": x["attn_b_wv"], "wo_b": x["attn_b_wo"].T,
        "w_r": x["ffn_W_r"].T, "w_k": x["ffn_W_k"].T, "w_v": x["ffn_W_v"].T,
        "mu_r": x["ffn_mu_r"].reshape(P, 1), "mu_k": x["ffn_mu_k"].reshape(P, 1),
        **tables(),
    }
    fed = {"x": x["attn_a_x"], "decay": arrays["decay"], "causal": arrays["causal"],
           "w_up": np.stack([x["attn_a_W_up_k"][:, cols], x["attn_a_W_up_v"]], axis=1),
           "norm_sum": arrays["norm_sum"].astype(mybir.dt.np(BF16))}
    for pack, members in PACKS.items():
        fed["pack_" + pack] = np.concatenate([arrays[name] for name, _ in members], axis=1)
    fed = {k: np.ascontiguousarray(v) for k, v in fed.items()}
    nc = bacc.Bacc("TRN2", target_bir_lowering=False, num_devices=1)
    dram = {k: nc.dram_tensor(k + "_dram", v.shape, mybir.dt.from_np(v.dtype), kind="ExternalInput").ap()
            for k, v in fed.items()}
    out = nc.dram_tensor("out_0_dram", (B, S, P), F32, kind="ExternalOutput").ap()
    build(nc, dram, out)
    result = run_bass_kernel_spmd(nc, [{k + "_dram": v for k, v in fed.items()}], core_ids=[0])
    return result.results[0]["out_0_dram"]
```
